# Optimizing a Trainium2 kernel written in Bass

```python
import numpy as np
import jax
import jax.numpy as jnp

def _softmax(x, axis=-1):
    return jax.nn.softmax(x, axis=axis)

def _gelu(x):
    return jax.nn.gelu(x, approximate=True)

def _silu(x):
    return jax.nn.silu(x)

def _sigmoid(x):
    return jax.nn.sigmoid(x)

def _layernorm(x, axis=-1, eps=1e-05):
    m = jnp.mean(x, axis=axis, keepdims=True)
    v = jnp.var(x, axis=axis, keepdims=True)
    return (x - m) / jnp.sqrt(v + eps)

def _scatter_add(tgt, idx, src, axis=0):
    return tgt.at[idx].add(src)

def _segment_sum(src, seg, n):
    return jax.ops.segment_sum(src, seg, n)
kernel_name = 'mk_xattn_seq_d1_seqx_r4_860e7f'

def setup_inputs(seed: int=0):
    np.random.seed(seed)
    _w = jnp.asarray

    def _rec_inputs():
        import jax
        import jax.numpy as jnp
        _rk = jax.random.key(seed)
        x = -0.000296 + 1 * jax.random.normal(jax.random.fold_in(_rk, 1), (8, 256, 320), jnp.float32)
        _lenS = 256 - jax.random.randint(jax.random.fold_in(_rk, 7), (8,), 0, max(1, 256 // 4) + 1, jnp.int32)
        _lenS2 = 120 - jax.random.randint(jax.random.fold_in(_rk, 8), (8,), 0, max(1, 120 // 4) + 1, jnp.int32)
        _ctx_2048P = jax.random.normal(jax.random.fold_in(_rk, 11), (8, 16, 512), jnp.float32)
        _ctx_2048c = jax.random.dirichlet(jax.random.fold_in(_rk, 511), 0.3 * jnp.ones((16,), jnp.float32), (8, 120))
        _ctx_2048t = jnp.einsum('bsk,bkd->bsd', _ctx_2048c, _ctx_2048P)
        _ctx_2048t = _ctx_2048t * jax.lax.rsqrt(jnp.mean(jnp.square(_ctx_2048t)) + 1e-12) * 0.953939
        ctx_2048 = 0.00118529 + 0.99962 * (_ctx_2048t + 0.3 * jax.random.normal(jax.random.fold_in(_rk, 611), (8, 120, 512), jnp.float32))
        fside_Bx4x4_0 = jax.random.uniform(jax.random.fold_in(_rk, 12), (8, 4, 4), jnp.float32, 0.0, 0.981965)
        return (x, ctx_2048, fside_Bx4x4_0)
    x, ctx_2048, fside_Bx4x4_0 = _rec_inputs()

    def _L0_xattn_setup():
        import jax, jax.numpy as jnp
        import numpy as np
        HEADS = 20
        NUM_IP_TOKENS = 4
        NUM_DUMMY_TOKENS = 4
        IP_SCALE = 1.0
        ASPECT_RATIO = 1.0
        NEG = -10000.0

        def _grid_hw(seq_len, aspect_ratio):
            width = int((seq_len / aspect_ratio) ** 0.5)
            height = seq_len // width
            while width * height != seq_len:
                if width * height < seq_len:
                    width += 1
                else:
                    width -= 1
                height = seq_len // width
            return (height, width)

        def _sdpa(q, k, v, mask=None):
            dh = q.shape[-1]
            scores = jnp.einsum('bhqd,bhkd->bhqk', q, k) / jnp.sqrt(jnp.asarray(dh, q.dtype))
            if mask is not None:
                scores = scores + mask
            probs = jax.nn.softmax(scores, axis=-1)
            return jnp.einsum('bhqk,bhkd->bhqd', probs, v)

        def _split_heads(x, heads):
            b, l, d = x.shape
            return x.reshape(b, l, heads, d // heads).transpose(0, 2, 1, 3)

        def _merge_heads(x):
            b, h, l, dh = x.shape
            return x.transpose(0, 2, 1, 3).reshape(b, l, h * dh)

        def _ip_mask(bbox, batch_size, seq_len, dtype):
            M = bbox.shape[1]
            height, width = _grid_hw(seq_len, ASPECT_RATIO)
            x = jnp.linspace(0.0, 1.0, width, dtype=dtype)
            y = jnp.linspace(0.0, 1.0, height, dtype=dtype)
            yg, xg = jnp.meshgrid(y, x, indexing='ij')
            xg = xg.reshape(-1)
            yg = yg.reshape(-1)
            x1, y1, x2, y2 = (bbox[..., 0:1], bbox[..., 1:2], bbox[..., 2:3], bbox[..., 3:4])
            inside = (xg >= x1) & (xg <= x2) & (yg >= y1) & (yg <= y2)
            ip_mask = jnp.where(inside, 0.0, NEG).astype(dtype)
            ip_mask = jnp.transpose(ip_mask, (0, 2, 1))[:, None]
            ip_mask = jnp.repeat(ip_mask, NUM_IP_TOKENS // M, axis=-1)
            dummy = jnp.where(jnp.any(inside, axis=1), NEG, 0.0).astype(dtype)
            dummy = jnp.repeat(dummy[:, None, :, None], NUM_DUMMY_TOKENS, axis=-1)
            return jnp.concatenate([dummy, ip_mask], axis=-1)
        key = jax.random.key(seed)
        ks = jax.random.split(key, 12)
        B, S, D, C = (4, 1024, 320, 512)
        text_len, M = (77, 4)
        hidden_states = jax.random.normal(ks[0], (B, S, D), jnp.float32)
        encoder_hidden_states = jax.random.normal(ks[1], (B, text_len + NUM_IP_TOKENS + NUM_DUMMY_TOKENS, C), jnp.float32)
        p1 = jax.random.uniform(ks[2], (B, M, 2), jnp.float32)
        p2 = jax.random.uniform(ks[3], (B, M, 2), jnp.float32)
        bbox = jnp.concatenate([jnp.minimum(p1, p2), jnp.maximum(p1, p2)], axis=-1)
        s = 0.02
        w_q = jax.random.normal(ks[4], (D, D), jnp.float32) * s
        w_k = jax.random.normal(ks[5], (C, D), jnp.float32) * s
        w_v = jax.random.normal(ks[6], (C, D), jnp.float32) * s
        w_k_ip = jax.random.normal(ks[7], (C, D), jnp.float32) * s
        w_v_ip = jax.random.normal(ks[8], (C, D), jnp.float32) * s
        w_out = jax.random.normal(ks[9], (D, D), jnp.float32) * s
        b_out = jnp.zeros((D,), jnp.float32)
        return {'hidden_states': hidden_states, 'encoder_hidden_states': encoder_hidden_states, 'bbox': bbox, 'w_q': w_q, 'w_k': w_k, 'w_v': w_v, 'w_k_ip': w_k_ip, 'w_v_ip': w_v_ip, 'w_out': w_out, 'b_out': b_out}
    _L0_xattn_all = _L0_xattn_setup()
    _L0_xattn_in = {k: v for k, v in _L0_xattn_all.items() if k in ('w_q', 'w_k', 'w_v', 'w_k_ip', 'w_v_ip', 'w_out', 'b_out')}
    del _L0_xattn_all
    return {'x': x, 'ctx_2048': ctx_2048, 'fside_Bx4x4_0': fside_Bx4x4_0, 'L0_xattn_w_q': _L0_xattn_in['w_q'], 'L0_xattn_w_k': _L0_xattn_in['w_k'], 'L0_xattn_w_v': _L0_xattn_in['w_v'], 'L0_xattn_w_k_ip': _L0_xattn_in['w_k_ip'], 'L0_xattn_w_v_ip': _L0_xattn_in['w_v_ip'], 'L0_xattn_w_out': _L0_xattn_in['w_out'], 'L0_xattn_b_out': _L0_xattn_in['b_out']}

def reference(x, ctx_2048, fside_Bx4x4_0, L0_xattn_w_q, L0_xattn_w_k, L0_xattn_w_v, L0_xattn_w_k_ip, L0_xattn_w_v_ip, L0_xattn_w_out, L0_xattn_b_out):
    import jax
    import jax.numpy as jnp

    def _L0_xattn_ref(hidden_states, encoder_hidden_states, bbox, w_q, w_k, w_v, w_k_ip, w_v_ip, w_out, b_out):
        import jax, jax.numpy as jnp
        import numpy as np
        HEADS = 20
        NUM_IP_TOKENS = 4
        NUM_DUMMY_TOKENS = 4
        IP_SCALE = 1.0
        ASPECT_RATIO = 1.0
        NEG = -10000.0

        def _grid_hw(seq_len, aspect_ratio):
            width = int((seq_len / aspect_ratio) ** 0.5)
            height = seq_len // width
            while width * height != seq_len:
                if width * height < seq_len:
                    width += 1
                else:
                    width -= 1
                height = seq_len // width
            return (height, width)

        def _sdpa(q, k, v, mask=None):
            dh = q.shape[-1]
            scores = jnp.einsum('bhqd,bhkd->bhqk', q, k) / jnp.sqrt(jnp.asarray(dh, q.dtype))
            if mask is not None:
                scores = scores + mask
            probs = jax.nn.softmax(scores, axis=-1)
            return jnp.einsum('bhqk,bhkd->bhqd', probs, v)

        def _split_heads(x, heads):
            b, l, d = x.shape
            return x.reshape(b, l, heads, d // heads).transpose(0, 2, 1, 3)

        def _merge_heads(x):
            b, h, l, dh = x.shape
            return x.transpose(0, 2, 1, 3).reshape(b, l, h * dh)

        def _ip_mask(bbox, batch_size, seq_len, dtype):
            M = bbox.shape[1]
            height, width = _grid_hw(seq_len, ASPECT_RATIO)
            x = jnp.linspace(0.0, 1.0, width, dtype=dtype)
            y = jnp.linspace(0.0, 1.0, height, dtype=dtype)
            yg, xg = jnp.meshgrid(y, x, indexing='ij')
            xg = xg.reshape(-1)
            yg = yg.reshape(-1)
            x1, y1, x2, y2 = (bbox[..., 0:1], bbox[..., 1:2], bbox[..., 2:3], bbox[..., 3:4])
            inside = (xg >= x1) & (xg <= x2) & (yg >= y1) & (yg <= y2)
            ip_mask = jnp.where(inside, 0.0, NEG).astype(dtype)
            ip_mask = jnp.transpose(ip_mask, (0, 2, 1))[:, None]
            ip_mask = jnp.repeat(ip_mask, NUM_IP_TOKENS // M, axis=-1)
            dummy = jnp.where(jnp.any(inside, axis=1), NEG, 0.0).astype(dtype)
            dummy = jnp.repeat(dummy[:, None, :, None], NUM_DUMMY_TOKENS, axis=-1)
            return jnp.concatenate([dummy, ip_mask], axis=-1)
        B, S, D = hidden_states.shape
        residual = hidden_states
        end_pos = encoder_hidden_states.shape[1] - (NUM_IP_TOKENS + NUM_DUMMY_TOKENS)
        text = encoder_hidden_states[:, :end_pos]
        ip_h = encoder_hidden_states[:, end_pos:]
        q = _split_heads(hidden_states @ w_q, HEADS)
        k = _split_heads(text @ w_k, HEADS)
        v = _split_heads(text @ w_v, HEADS)
        out_text = _sdpa(q, k, v)
        out_text = _merge_heads(out_text)
        mask_ip = _ip_mask(bbox, B, S, hidden_states.dtype)
        k_ip = _split_heads(ip_h @ w_k_ip, HEADS)
        v_ip = _split_heads(ip_h @ w_v_ip, HEADS)
        out_ip = _merge_heads(_sdpa(q, k_ip, v_ip, mask=mask_ip))
        out = out_text + IP_SCALE * out_ip
        out = out @ w_out + b_out
        out = out + residual
        return out
    x = _L0_xattn_ref(x, ctx_2048, fside_Bx4x4_0, L0_xattn_w_q, L0_xattn_w_k, L0_xattn_w_v, L0_xattn_w_k_ip, L0_xattn_w_v_ip, L0_xattn_w_out, L0_xattn_b_out)
    return x

_drawn_inputs = setup_inputs


def setup_inputs(seed=0):
    import zlib

    import numpy as np

    out = dict(_drawn_inputs(seed))
    spreads = {'L0_xattn_b_out': (0.0, 0.1)}
    factors = {'L0_xattn_w_q': 5.564, 'L0_xattn_w_k': 8.0, 'L0_xattn_w_k_ip': 6.296}
    for name, (base, spread) in spreads.items():
        noise = np.random.default_rng([zlib.crc32(name.encode()), seed]).standard_normal(out[name].shape)
        drawn = base * np.exp(spread * noise) if base else spread * noise
        out[name] = jnp.asarray(drawn.astype(out[name].dtype))
    for name, factor in factors.items():
        out[name] = (out[name] * factor).astype(out[name].dtype)
    return out
```

```python
from contextlib import ExitStack

import concourse.bass as bass
from concourse import mybir

F32 = mybir.dt.float32
F32R = mybir.dt.float32r
ALU = mybir.AluOpType
ACT = mybir.ActivationFunctionType
X = mybir.AxisListType.X

P = 128
B, S, D, C = 8, 256, 320, 512
H, DH = 20, 16
TEXT, IP = 112, 8
KEYS = TEXT + IP
BOX = IP // 2
GRID = 16
PAIRS = H // 2
QT = S // P
CC = C // P
XC = 3
DP = XC * P
GROUP = 4
GROUPS = H // GROUP
HPC = P // DH
SCALE = float(DH) ** -0.5
NEG = -10000.0 / SCALE
STACK = 3 * 32
SHIFT = 4

IDENT = 0
XG = IDENT + P
YG = XG + 1
NEG_SECOND = YG + QT
NEG_LOWER = NEG_SECOND + 1
SHIFT_ROWS = NEG_LOWER + 1
SUM_COLS = SHIFT_ROWS + 2
BLOCK = SUM_COLS + 3 * 32
CONSTS = BLOCK + DP


def constants():
    import numpy as np

    c = np.zeros((P, CONSTS), np.float32)
    p = np.arange(P)
    c[:, IDENT:IDENT + P] = np.eye(P)
    lin = np.linspace(0.0, 1.0, GRID, dtype=np.float32)
    c[:, XG] = lin[p % GRID]
    for t in range(QT):
        c[:, YG + t] = lin[(t * P + p) // GRID]
    c[:, NEG_SECOND] = -1.0 * (p % 32 >= DH)
    c[:, NEG_LOWER] = -1.0 * (p >= 64)
    for r in range(SHIFT):
        c[STACK + r, SHIFT_ROWS + r % 2] = 1.0
    c[:, SUM_COLS:SUM_COLS + DH] = 1.0
    c[:, SUM_COLS + 32 + DH:SUM_COLS + 64] = 1.0
    c[:, SUM_COLS + 64:SUM_COLS + 96] = 1.0
    head = p % (HPC * IP) // IP
    for j in range(XC):
        d = np.arange(P)
        own = d // DH if j < 2 else d // 32
        c[:, BLOCK + j * P:BLOCK + (j + 1) * P] = head[:, None] == own[None, :]
    return c


def build(nc, xT, x, ctxT, ctx_ipT, bbox, wq, wk, wv, wk_ip, wv_ip, w_out, b_out, consts, out):
    ctx = ExitStack()
    with ctx:
        def sb(name, shape, dt=F32):
            return ctx.enter_context(nc.sbuf_tensor(name, shape, dt))

        def sem(name):
            return ctx.enter_context(nc.semaphore(name))

        k_dram = nc.dram_tensor("k_dram", (2, PAIRS, 2, DH, B, KEYS), F32, kind="Internal").ap()
        vip_dram = nc.dram_tensor("vip_dram", (HPC, IP, B, DP), F32, kind="Internal").ap()
        q_dram = nc.dram_tensor("q_dram", (2, DP // 32, 32, S), F32, kind="Internal").ap()

        shift_dram = nc.dram_tensor("shift_dram", (2, 2, PAIRS, S), F32, kind="Internal").ap()

        con = sb("con", [P, CONSTS])
        ident = con[:, IDENT:IDENT + P]
        raw = sb("raw", [P, PAIRS * 2 * S + B * D])
        w_raw = raw[:, 0:2 * CC * DP].rearrange("p (s j n) -> p s j n", s=2, j=CC)
        ctx_raw = raw[:, 2 * CC * DP:2 * CC * DP + CC * B * TEXT].rearrange("p (j n) -> p j n", j=CC)
        probs = raw[0:TEXT, 0:PAIRS * 2 * S].rearrange("p (a n) -> p a n", a=PAIRS)
        v_all = raw[0:TEXT, PAIRS * 2 * S:].rearrange("p (b h d) -> p b h d", b=B, h=H)
        ctx_hl = sb("ctx_hl", [P, 2, CC * B * TEXT], F32R)
        ctx_h, ctx_l = (ctx_hl[:, n].rearrange("p (j n) -> p j n", j=CC) for n in range(2))
        vr = ctx_hl[:, 0, 0:B * DP].bitcast(F32).rearrange("p (b n) -> p b n", b=B)
        cip_raw = sb("cip_raw", [P, CC, P])
        cip_h, cip_l = (sb(n, [P, CC, P], F32R) for n in ("cip_h", "cip_l"))
        key_w = sb("key_w", [P, 4, CC * DP], F32R)
        wk_h, wk_l, wkip_h, wkip_l = (key_w[:, n].rearrange("p (j n) -> p j n", j=CC) for n in range(4))
        key_w_flat = key_w[:].rearrange("p s n -> p (s n)")
        wq_h, wq_l = (sb(n, [P, XC, DP], F32R) for n in ("wq_h", "wq_l"))
        wv_h, wv_l = (sb(n, [P, CC, D], F32R) for n in ("wv_h", "wv_l"))
        wo_h, wo_l = (sb(n, [P, XC, D], F32R) for n in ("wo_h", "wo_l"))
        late = sb("late", [P, 3 * XC * S + 2 * QT * D + 2 * S])
        ot, oi, on = (late[:, n * XC * S:(n + 1) * XC * S].rearrange("p (c n) -> p c n", c=XC) for n in range(3))
        at_x = 3 * XC * S
        x_res, y = (late[:, at_x + n * QT * D:at_x + (n + 1) * QT * D].rearrange("p (t n) -> p t n", t=QT)
                    for n in range(2))
        rz = late[:, at_x + 2 * QT * D:].rearrange("p (k n) -> p k n", k=2)
        kc_more = sb("kc_more", [P, 2, B * KEYS])
        kc = [late[:, n * B * KEYS:(n + 1) * B * KEYS] for n in range(4)] + [kc_more[:, n] for n in range(2)]
        kc = [t.bitcast(F32R).rearrange("p (b n) -> p b n", b=B) for t in kc]
        kc_h, kc_l = kc[0:XC], kc[XC:]
        box = sb("box", [P, B, BOX, 4])
        inside = sb("inside", [P, QT, B, BOX])
        some = sb("some", [P, QT, B])
        mask = sb("mask", [P, QT, B, IP])
        bias = sb("bias", [P, D])

        x_raw = sb("x_raw", [P, XC, S])
        x_h, x_l = (sb(n, [P, XC, S], F32R) for n in ("x_h", "x_l"))
        q_h, q_l = (sb(n, [P, XC, S], F32R) for n in ("q_h", "q_l"))
        qs = [sb("qs0", [P, PAIRS, S], F32R),
              key_w_flat[:, 0:PAIRS * S].rearrange("p (a n) -> p a n", a=PAIRS)]
        ks = [sb("ks0", [P, PAIRS, 2, KEYS], F32R),
              key_w_flat[:, 2 * CC * DP:2 * CC * DP + PAIRS * 2 * KEYS].rearrange("p (a s n) -> p a s n", a=PAIRS, s=2)]
        v = [sb(f"v{k}", [TEXT, H, 32]) for k in range(2)]
        negmax = sb("negmax", [P, QT, 2, PAIRS])
        shift = sb("shift", [H, 2, S], F32R)
        ips = sb("ips", [P, QT, H, IP])
        ipd = sb("ipd", [P, QT, H, IP])
        ipe = sb("ipe", [P, QT, H, IP])
        ipm = sb("ipm", [P, QT, H])
        ipz = sb("ipz", [P, QT, H])
        ipr = sb("ipr", [P, QT, H])
        ipp = sb("ipp", [P, QT, XC * HPC, IP])
        pip = sb("pip", [P, XC, S], F32R)
        vipn = sb("vipn", [B * IP, DP])
        vm = sb("vm", [P, DP])
        vip_h, vip_l = (sb(n, [P, DP], F32R) for n in ("vip_h", "vip_l"))
        on_h, on_l = (sb(n, [P, XC, S], F32R) for n in ("on_h", "on_l"))
        xb = sb("xb", [P, QT, D])

        bank = [ctx.enter_context(nc.psum_tensor(f"bank{i}", [P, 512], F32)) for i in range(8)]
        a_bank = bank[0:2]
        b_bank = bank[2:4]
        oz_bank = bank[4:6]
        spare = bank[6:8]

        wk_ctx_in = [sem(f"wk_ctx_in{j}") for j in range(CC)]
        kip_in, vip_w_in, wq_in, wv_in, wo_in = (sem(n) for n in ("kip_in", "vip_w_in", "wq_in", "wv_in", "wo_in"))
        con_in, box_in, bias_in = (sem(n) for n in ("con_in", "box_in", "bias_in"))
        x_in, xres_in, ks_in, vr_in = (sem(n) for n in ("x_in", "xres_in", "ks_in", "vr_in"))
        high, low = sem("high"), sem("low")
        zeroed, ones_set, mask_ready, mask_step = (sem(n) for n in ("zeroed", "ones_set", "mask_ready", "mask_step"))
        k_ready, kh_done, kl_done, k_stored = (sem(n) for n in ("k_ready", "kh_done", "kl_done", "k_stored"))
        vipn_ready, vipn_done, vipn_stored = (sem(n) for n in ("vipn_ready", "vipn_done", "vipn_stored"))
        xh_done, xl_done = sem("xh_done"), sem("xl_done")
        q_ready, qh_done, ql_done, q_stored, qs_in = (
            sem(n) for n in ("q_ready", "qh_done", "ql_done", "q_stored", "qs_in"))
        va_ready, va_done, v_done = sem("va_ready"), sem("va_done"), sem("v_done")
        a_ready, a_max, a_used = sem("a_ready"), sem("a_max"), sem("a_used")
        shift_ready, sh_done, sl_done, shift_in = (sem(n) for n in ("shift_ready", "sh_done", "sl_done", "shift_in"))
        shift_stored = sem("shift_stored")
        ipm_done, ipd_done, ipe_done, ipz_done, ipr_done, ipp_done = (
            sem(n) for n in ("ipm_done", "ipd_done", "ipe_done", "ipz_done", "ipr_done", "ipp_done"))
        ipt_ready, pih_done, pil_done = sem("ipt_ready"), sem("pih_done"), sem("pil_done")
        vm_done, viph_done, vip_done = sem("vm_done"), sem("viph_done"), sem("vip_done")
        oip_ready, oi_done = sem("oip_ready"), sem("oi_done")
        b_ready, p_done, oz_ready = sem("b_ready"), sem("p_done"), sem("oz_ready")
        rz_done, ot_done, on_done, onh_done, onl_done = (
            sem(n) for n in ("rz_done", "ot_done", "on_done", "onh_done", "onl_done"))
        out_ready, xb_done, y_done, y_stored = (sem(n) for n in ("out_ready", "xb_done", "y_done", "y_stored"))

        splits = []
        for j in range(CC):
            splits.append((wk_ctx_in[j], 32, wk_h[:, j, :], wk_l[:, j, :], w_raw[:, 0, j, :]))
            splits.append((wk_ctx_in[j], 32, ctx_h[:, j, :], ctx_l[:, j, :], ctx_raw[:, j, :]))
        splits.append((kip_in, 32, cip_h[:], cip_l[:], cip_raw[:]))
        splits.append((kip_in, 32, wkip_h[:], wkip_l[:], w_raw[:, 1]))
        K_SPLIT = len(splits)
        splits.append((wq_in, 16, wq_h[:], wq_l[:], w_raw[:, 0, 0:XC, :]))
        Q_SPLIT = len(splits)
        splits.append((wv_in, 16, wv_h[:], wv_l[:], w_raw[:, 1, :, 0:D]))
        V_SPLIT = len(splits)
        splits.append((vip_w_in, 16, wkip_h[:], wkip_l[:], ctx_raw[:, :, 0:DP]))
        VIP_SPLIT = len(splits)
        splits.append((wo_in, 16, wo_h[:], wo_l[:], ctx_raw[:, 0:XC, DP:DP + D]))
        wo_raw = ctx_raw[:, 0:XC, DP:DP + D]
        wvip_h, wvip_l, wvip_raw = wkip_h, wkip_l, ctx_raw[:, :, 0:DP]

        def chunk_heads(c):
            if c < 2:
                return [(j, 4 * c + j, ab, ab) for ab in range(2) for j in range(4)]
            return [(j, 8 + j // 2, j % 2, 2) for j in range(4)]

        block = ctx.enter_context(nc.Block())

        @block.sync
        def _(sp):
            for j in range(CC):
                sp.dma_start(w_raw[:, 0, j, :], wk[:, j, :]).then_inc(wk_ctx_in[j], 16)
                sp.dma_start(ctx_raw[:, j, :], ctxT[:, j, :]).then_inc(wk_ctx_in[j], 16)
            sp.dma_start(cip_raw[:], ctx_ipT).then_inc(kip_in, 16)
            sp.dma_start(w_raw[:, 1], wk_ip).then_inc(kip_in, 16)
            sp.dma_start(con[:], consts).then_inc(con_in, 16)
            sp.dma_start(x_raw[:], xT[0]).then_inc(x_in, 16)
            sp.dma_start(box[:].rearrange("p b m c -> p (b m c)"), bbox.partition_broadcast(P)).then_inc(box_in, 16)
            sp.dma_start(bias[:], b_out.partition_broadcast(P)).then_inc(bias_in, 16)
            sp.wait_ge(high, 2 * CC)
            sp.wait_ge(low, 2 * CC)
            sp.dma_start(w_raw[:, 0, 0:XC, :], wq).then_inc(wq_in, 16)
            sp.dma_start(ctx_raw[:, :, 0:DP], wv_ip).then_inc(vip_w_in, 16)
            sp.dma_start(wo_raw, w_out).then_inc(wo_in, 16)
            sp.wait_ge(high, K_SPLIT)
            sp.wait_ge(low, K_SPLIT)
            sp.dma_start(w_raw[:, 1, :, 0:D], wv).then_inc(wv_in, 16)

            sp.wait_ge(kh_done, 7)
            sp.wait_ge(kl_done, 7)
            for part, kc_part in enumerate((kc_h, kc_l)):
                rows = k_dram[part].rearrange("p a d b n -> (p a d) (b n)")
                for m in range(XC):
                    n = min(P, D - m * P)
                    sp.dma_start(rows[m * P:m * P + n, :],
                                 kc_part[m][0:n].bitcast(F32).rearrange("p b n -> p (b n)")).then_inc(k_stored, 16)
            sp.wait_ge(vipn_done, 1)
            sp.dma_start(vip_dram.rearrange("h k b n -> (k b) h n"),
                         vipn[:].unsqueeze(1).to_broadcast([B * IP, HPC, DP])).then_inc(vipn_stored, 16)
            sp.wait_ge(k_stored, 16 * 2 * XC)
            sp.wait_ge(vipn_stored, 16)

            def stage(c, k, reuse):
                if reuse:
                    sp.wait_ge(b_ready, PAIRS * (c - 1))
                for blk, part in enumerate((0, 1, 0)):
                    for ab in range(2):
                        r = 32 * blk + DH * ab
                        sp.dma_start(ks[k][r:r + DH, :, ab, :].bitcast(F32),
                                     k_dram[part, :, ab, :, c, :].rearrange("p d n -> d p n")).then_inc(ks_in, 16)

            def queries(c, k):
                if not (isinstance(c, int) and c == 0):
                    sp.wait_ge(qs_in, 16 * 3 * c)
                for part, (done, tile) in enumerate(((qh_done, q_h), (ql_done, q_l))):
                    sp.wait_ge(done, 2 * (c + 1))
                    sp.dma_start(q_dram[part].rearrange("(m j) r n -> (j r) m n", m=XC),
                                 tile[:].bitcast(F32)).then_inc(q_stored, 16)
                sp.wait_ge(q_stored, 16 * 2 * (c + 1))
                for blk, part in enumerate((0, 0, 1)):
                    sp.dma_start(qs[k][32 * blk:32 * blk + 32, :, :].bitcast(F32),
                                 q_dram[part, 0:PAIRS].rearrange("a r n -> r a n")).then_inc(qs_in, 16)

            def shifts(c, k):
                if not (isinstance(c, int) and c == 0):
                    sp.wait_ge(shift_in, 16 * c)
                sp.wait_ge(sh_done, c + 1)
                sp.wait_ge(sl_done, c + 1)
                sp.dma_start(shift_dram.rearrange("s a p n -> (a p) s n"),
                             shift[:].bitcast(F32)).then_inc(shift_stored, 16)
                sp.wait_ge(shift_stored, 16 * (c + 1))
                sp.dma_start(qs[k][STACK:STACK + SHIFT, :, :].bitcast(F32),
                             shift_dram.rearrange("s a p n -> (s a) p n")).then_inc(shift_in, 16)

            def store(b):
                sp.wait_ge(y_done, QT * (b + 1))
                sp.dma_start(out[b].rearrange("(t p) d -> p t d", p=P), y[:]).then_inc(y_stored, 16)

            def residual(b, reuse):
                if reuse:
                    sp.wait_ge(xb_done, b)
                sp.dma_start(x_res[:], x[b].rearrange("(t p) d -> p t d", p=P)).then_inc(xres_in, 16)

            def step(b, k, first=False, last=False):
                residual(b, not first)
                if not last:
                    stage(b + 1, 1 - k, not first)
                    sp.wait_ge(xl_done, 2 * (b + 2))
                    sp.wait_ge(xh_done, b + 2)
                    sp.dma_start(x_raw[:], xT[b + 2]).then_inc(x_in, 16)
                    queries(b + 1, 1 - k)
                if not first:
                    store(b - 1)
                if not last:
                    shifts(b + 1, 1 - k)

            sp.wait_ge(zeroed, 5)
            stage(0, 0, False)
            sp.wait_ge(xh_done, 1)
            sp.wait_ge(xl_done, 2)
            sp.dma_start(x_raw[:], xT[1]).then_inc(x_in, 16)
            queries(0, 0)
            sp.wait_ge(va_ready, B)
            for half in range(2):
                sp.dma_start(vr[64 * half:64 * half + 64],
                             vip_dram.rearrange("h k b n -> (h k) b n")).then_inc(vr_in, 16)
            shifts(0, 0)
            step(0, 0, first=True)
            with sp.Fori(0, (B - 2) // 2) as i:
                step(2 * i + 1, 1)
                step(2 * i + 2, 0)
            step(B - 1, 1, last=True)
            store(B - 1)
            sp.wait_ge(y_stored, 16 * B)

        @block.tensor
        def _(pe):
            def three(out_ap, products, start=True, stop=True):
                for n, (lhsT, rhs) in enumerate(products):
                    mm = pe.matmul(out_ap, lhsT, rhs, start=start and n == 0, stop=stop and n == len(products) - 1)
                return mm

            for j in range(CC):
                pe.wait_ge(high, 2 * j + 2)
                pe.wait_ge(low, 2 * j + 2)
                for m in range(XC):
                    w_hi, w_lo = (w[:, j, m * P:(m + 1) * P] for w in (wk_h, wk_l))
                    for half in range(2):
                        n = slice(half * 448, half * 448 + 448)
                        mm = three(bank[2 * m + half][:, 0:448],
                                   [(w_hi, ctx_h[:, j, n]), (w_hi, ctx_l[:, j, n]), (w_lo, ctx_h[:, j, n])],
                                   start=j == 0, stop=j == CC - 1)
                        if j == CC - 1:
                            mm.then_inc(k_ready, 1)
            pe.wait_ge(high, K_SPLIT)
            pe.wait_ge(low, K_SPLIT)
            for m in range(XC):
                mm = three(spare[0][:, 64 * m:64 * m + 64],
                           [(w[:, j, m * P:(m + 1) * P], t[:, j, 0:B * IP]) for j in range(CC)
                            for w, t in ((wkip_h, cip_h), (wkip_h, cip_l), (wkip_l, cip_h))])
            mm.then_inc(k_ready, 1)
            pe.wait_ge(high, VIP_SPLIT)
            pe.wait_ge(low, VIP_SPLIT)
            three(spare[1][:, 0:DP],
                  [(t[:, j, :], w[:, j, :]) for j in range(CC)
                   for t, w in ((cip_h, wvip_h), (cip_h, wvip_l), (cip_l, wvip_h))]).then_inc(vipn_ready, 1)

            def project_q(c):
                pe.wait_ge(xh_done, c + 1)
                pe.wait_ge(xl_done, 2 * (c + 1))
                for m in range(XC):
                    cols = slice(m * P, (m + 1) * P)
                    prods = [(w[:, j, cols], t[:, j, :]) for j in range(2)
                             for w, t in ((wq_h, x_h), (wq_h, x_l), (wq_l, x_h))]
                    prods += [(wq_h[:, 2, cols], x_l[:, 2, :]), (wq_l[:, 2, cols], x_l[:, 2, :])]
                    mm = three(spare[m // 2][:, S * (m % 2):S * (m % 2) + S], prods)
                    if m:
                        mm.then_inc(q_ready, 1)

            def project_v(b):
                n = slice(b * TEXT, (b + 1) * TEXT)
                three(bank[b][0:TEXT, 0:D],
                      [(t[:, j, n], w[:, j, :]) for j in range(CC)
                       for t, w in ((ctx_h, wv_h), (ctx_h, wv_l), (ctx_l, wv_h))]).then_inc(va_ready, 1)

            def score_a(c, k, n):
                if n == 0:
                    pe.wait_ge(qs_in, 16 * 3 * (c + 1))
                    pe.wait_ge(ks_in, 16 * 6 * (c + 1))
                t, g = n // GROUPS, n % GROUPS
                if n >= 2 or not (isinstance(c, int) and c == 0):
                    pe.wait_ge(a_used, 2 * GROUPS * c + n - 1)
                for p in range(2):
                    mm = pe.matmul(a_bank[n % 2][:, 2 * KEYS * p:2 * KEYS * (p + 1)],
                                   qs[k][0:STACK, 2 * g + p, t * P:(t + 1) * P],
                                   ks[k][0:STACK, 2 * g + p, :, :].rearrange("p a n -> p (a n)"),
                                   start=True, stop=True)
                mm.then_inc(a_ready, 1)

            def transpose_max(c):
                pe.wait_ge(a_max, 2 * GROUPS * (c + 1))
                for t in range(QT):
                    mm = pe.transpose(spare[1][0:H, t * P:(t + 1) * P], negmax[:, t].rearrange("p a n -> p (a n)"), ident)
                mm.then_inc(shift_ready, 1)

            def score_b(b, k, p):
                if p == 0:
                    pe.wait_ge(shift_in, 16 * (b + 1))
                if p >= 2 or not (isinstance(b, int) and b == 0):
                    pe.wait_ge(p_done, PAIRS * b + p - 1)
                for ab in range(2):
                    mm = pe.matmul(b_bank[p % 2][0:TEXT, S * ab:S * ab + S],
                                   ks[k][0:STACK + SHIFT, p, ab, 0:TEXT],
                                   qs[k][0:STACK + SHIFT, p, :], start=True, stop=True)
                mm.then_inc(b_ready, 1)

            def transpose_ip(b, part):
                if part == 0:
                    pe.wait_ge(ipp_done, b + 1)
                for c in (0, 1) if part == 0 else (2,):
                    for t in range(QT):
                        at = S * (c % 2) + t * P
                        mm = pe.transpose(spare[part][0:HPC * IP, at:at + P],
                                          ipp[:, t, HPC * c:HPC * (c + 1), :].rearrange("p h n -> p (h n)"), ident)
                mm.then_inc(ipt_ready, 1)

            def image_out(b, part):
                if part == 0:
                    pe.wait_ge(pih_done, 2 * (b + 1))
                    pe.wait_ge(pil_done, 2 * (b + 1))
                    pe.wait_ge(vip_done, b + 1)
                for c in (0, 1) if part == 0 else (2,):
                    cols = slice(c * P, (c + 1) * P)
                    mm = three(spare[1 - part][:, S * (c % 2):S * (c % 2) + S],
                               [(w[:, cols], pip[:, c, :]) for w in (vip_h, vip_l)])
                mm.then_inc(oip_ready, 1)

            def text_out(b, k, c):
                heads = chunk_heads(c)
                pe.wait_ge(p_done, PAIRS * b + (4, 8, 10)[c])
                if c == 0:
                    pe.wait_ge(v_done, b + 1)
                turn = (k + c) % 2
                if c == 2 or not (isinstance(b, int) and b == 0):
                    pe.wait_ge(ot_done, XC * b + c - 1)
                oz = oz_bank[turn]
                for what in range(2):
                    for n, (j, p, ab, cols) in enumerate(heads):
                        w = (v[k][:, 2 * p + ab, :],
                             con[0:TEXT, SUM_COLS + 32 * cols:SUM_COLS + 32 * cols + 32])[what]
                        mm = pe.matmul(oz[32 * j:32 * j + 32, S * what:S * what + S], w,
                                       probs[:, p, S * ab:S * ab + S],
                                       start=what == 0 and n < 4, stop=n >= len(heads) - 4,
                                       skip_group_check=True)
                mm.then_inc(oz_ready, 1)

            def project_out(b, t):
                if t == 0:
                    pe.wait_ge(onh_done, XC * (b + 1))
                    pe.wait_ge(onl_done, XC * (b + 1))
                q = slice(t * P, (t + 1) * P)
                prods = [(o[:, j, q], w[:, j, :]) for j in range(2)
                         for o, w in ((on_h, wo_h), (on_h, wo_l), (on_l, wo_h))]
                prods += [(on_l[:, 2, q], wo_h[:, 2, :]), (on_l[:, 2, q], wo_l[:, 2, :])]
                three(spare[1 - t][:, 0:D], prods).then_inc(out_ready, 1)

            def step(b, k, first=False, last=False):
                c = b + 1
                if not last:
                    pe.wait_ge(sl_done, b + 1)
                    if not first:
                        pe.wait_ge(oi_done, 2 * b)
                    project_q(c)
                pe.wait_ge(con_in, 16)
                if not last:
                    pe.wait_ge(ql_done, 2 * (c + 1))
                else:
                    pe.wait_ge(oi_done, 2 * b)
                transpose_ip(b, 0)
                transpose_ip(b, 1)
                pe.wait_ge(pil_done, 2 * (b + 1))
                score_b(b, k, 0)
                if not first:
                    project_out(b - 1, 0)
                    project_out(b - 1, 1)
                score_b(b, k, 1)
                if not first:
                    pe.wait_ge(y_done, QT * b - 1)
                image_out(b, 0)
                score_b(b, k, 2)
                a = 0

                def more_a(n):
                    for m in range(n):
                        if not last:
                            score_a(c, 1 - k, a + m)
                    return a + n

                a = more_a(1)
                score_b(b, k, 3)
                a = more_a(1)
                score_b(b, k, 4)
                a = more_a(1)
                text_out(b, k, 0)
                for p in (5, 6, 7):
                    score_b(b, k, p)
                    a = more_a(1)
                a = more_a(1)
                if not first:
                    pe.wait_ge(y_done, QT * b)
                image_out(b, 1)
                text_out(b, k, 1)
                for p in (8, 9):
                    score_b(b, k, p)
                    a = more_a(1)
                text_out(b, k, 2)
                a = more_a(1)
                if not last:
                    pe.wait_ge(oi_done, 2 * b + 1)
                    transpose_max(c)

            pe.wait_ge(high, Q_SPLIT)
            pe.wait_ge(low, Q_SPLIT)
            pe.wait_ge(kl_done, 7)
            pe.wait_ge(vipn_done, 1)
            project_q(0)
            pe.wait_ge(high, V_SPLIT)
            pe.wait_ge(low, V_SPLIT)
            for b in range(B):
                if b == 6:
                    pe.wait_ge(ql_done, 2)
                project_v(b)
            pe.wait_ge(va_done, B)
            pe.wait_ge(con_in, 16)
            for n in range(2 * GROUPS):
                score_a(0, 0, n)
            transpose_max(0)
            pe.wait_ge(low, len(splits))
            pe.wait_ge(ones_set, 4)
            step(0, 0, first=True)
            with pe.Fori(0, (B - 2) // 2) as i:
                step(2 * i + 1, 1)
                step(2 * i + 2, 0)
            step(B - 1, 1, last=True)
            project_out(B - 1, 0)
            project_out(B - 1, 1)

        @block.scalar
        def _(act):
            copy = nc.scalar.copy
            for n, (loaded, count, hi, _, raw) in enumerate(splits[:Q_SPLIT - 1]):
                act.wait_ge(loaded, count)
                copy(hi, raw).then_inc(high, 1)

            def split_x(c):
                act.wait_ge(x_in, 16 * (c + 1))
                copy(x_h[:], x_raw[:]).then_inc(xh_done, 1)

            split_x(0)
            for m in range(XC):
                for half in range(2):
                    act.wait_ge(k_ready, 2 * m + half + 1)
                    copy(kc_h[m][:, 4 * half:4 * half + 4, 0:TEXT],
                         bank[2 * m + half][:, 0:448].rearrange("p (b n) -> p b n", b=4)).then_inc(kh_done, 1)
            act.wait_ge(k_ready, 7)
            for m in range(XC):
                mm = copy(kc_h[m][:, :, TEXT:KEYS],
                          spare[0][:, 64 * m:64 * m + 64].rearrange("p (n b) -> p b n", b=B))
            mm.then_inc(kh_done, 1)
            for loaded, count, hi, _, raw in splits[Q_SPLIT - 1:]:
                act.wait_ge(loaded, count)
                if hi is splits[VIP_SPLIT - 1][2]:
                    act.wait_ge(k_ready, 7)
                copy(hi, raw).then_inc(high, 1)
            act.wait_ge(vipn_ready, 1)
            copy(vipn[:], spare[1][0:B * IP, 0:DP]).then_inc(vipn_done, 1)

            def high_q(c, part):
                act.wait_ge(q_ready, 2 * c + part + 1)
                if part == 0 and not (isinstance(c, int) and c == 0):
                    act.wait_ge(q_stored, 32 * c)
                if part == 0:
                    copy(q_h[:, 0:2, :], spare[0][:].rearrange("p (m n) -> p m n", m=2)).then_inc(qh_done, 1)
                else:
                    copy(q_h[:, 2, :], spare[1][:, 0:S]).then_inc(qh_done, 1)

            def values(c, k):
                if not (isinstance(c, int) and c < 2):
                    act.wait_ge(oz_ready, XC * (c - 1))
                src = v_all[:, c]
                copy(v[k][:, 0:16:2, 0:DH], src[:, 0:16:2, :])
                copy(v[k][:, 1:16:2, DH:32], src[:, 1:16:2, :])
                copy(v[k][:, 16:H, 0:DH], src[:, 16:H, :])
                copy(v[k][:, 16:H, DH:32], src[:, 16:H, :]).then_inc(v_done, 1)

            def high_shift(c):
                act.wait_ge(shift_ready, c + 1)
                if not (isinstance(c, int) and c == 0):
                    act.wait_ge(shift_stored, 16 * c)
                copy(shift[:, 0], spare[1][0:H, 0:S]).then_inc(sh_done, 1)

            def image_exp(c):
                act.wait_ge(ipd_done, c + 1)
                if not (isinstance(c, int) and c == 0):
                    act.wait_ge(ipp_done, c)
                nc.scalar.activation(ipe[:], ipd[:], ACT.Exp, scale=SCALE).then_inc(ipe_done, 1)

            def probabilities(b, p):
                act.wait_ge(b_ready, PAIRS * b + p + 1)
                if p in (0, 4, 8) and not (isinstance(b, int) and b == 0):
                    act.wait_ge(oz_ready, XC * (b - 1) + p // 4 + 1)
                nc.scalar.activation(probs[:, p, :], b_bank[p % 2][0:TEXT, :], ACT.Exp,
                                     scale=SCALE).then_inc(p_done, 1)

            def high_ip(b, part):
                act.wait_ge(ipt_ready, 2 * b + part + 1)
                if part == 0:
                    if not (isinstance(b, int) and b == 0):
                        act.wait_ge(oip_ready, 2 * b)
                    copy(pip[0:64, 0:2, :], spare[0][0:64, :].rearrange("p (m n) -> p m n", m=2)).then_inc(pih_done, 1)
                else:
                    copy(pip[0:64, 2, :], spare[1][0:64, 0:S]).then_inc(pih_done, 1)

            def image_part(b, part):
                act.wait_ge(oip_ready, 2 * b + part + 1)
                if part == 0:
                    if not (isinstance(b, int) and b == 0):
                        act.wait_ge(on_done, XC * b)
                    copy(oi[:, 0:2, :], spare[1][:].rearrange("p (m n) -> p m n", m=2)).then_inc(oi_done, 1)
                else:
                    copy(oi[:, 2, :], spare[0][:, 0:S]).then_inc(oi_done, 1)

            def high_out(b, c):
                act.wait_ge(on_done, XC * b + c + 1)
                if c == 0 and not (isinstance(b, int) and b == 0):
                    act.wait_ge(out_ready, QT * b)
                copy(on_h[:, c, :], on[:, c, :]).then_inc(onh_done, 1)

            def step(b, k, first=False, last=False):
                c = b + 1
                if not last:
                    high_q(c, 0)
                    high_q(c, 1)
                high_ip(b, 0)
                high_ip(b, 1)
                if not last:
                    values(c, 1 - k)
                probabilities(b, 0)
                probabilities(b, 1)
                if not last:
                    act.wait_ge(q_ready, 2 * (c + 1))
                    split_x(c + 1)
                image_part(b, 0)
                for p in range(2, 8):
                    probabilities(b, p)
                high_out(b, 0)
                image_part(b, 1)
                probabilities(b, 8)
                probabilities(b, 9)
                high_out(b, 1)
                if not last:
                    high_shift(c)
                    image_exp(c)
                high_out(b, 2)

            high_q(0, 0)
            high_q(0, 1)
            act.wait_ge(zeroed, 4)
            act.wait_ge(high, len(splits))
            act.wait_ge(low, len(splits))
            for b in range(B):
                act.wait_ge(va_ready, b + 1)
                copy(v_all[:, b], bank[b][0:TEXT, 0:D].rearrange("p (h d) -> p h d", h=H)).then_inc(va_done, 1)
            act.wait_ge(va_done, B)
            values(0, 0)
            act.wait_ge(q_ready, 2)
            split_x(1)
            high_shift(0)
            image_exp(0)
            step(0, 0, first=True)
            with act.Fori(0, (B - 2) // 2) as i:
                step(2 * i + 1, 1)
                step(2 * i + 2, 0)
            step(B - 1, 1, last=True)

        @block.vector
        def _(dve):
            sub = lambda o, a, b: nc.vector.tensor_tensor(o, a, b, ALU.subtract)

            def split_x(c):
                dve.wait_ge(xh_done, c + 1)
                nc.vector.scalar_tensor_tensor(x_l[:, 2, :], x_h[:, 2, :], con[:, NEG_LOWER:NEG_LOWER + 1],
                                               x_raw[:, 2, :], ALU.mult, ALU.add).then_inc(xl_done, 1)

            for n, (loaded, count, hi, lo, raw) in enumerate(splits[:Q_SPLIT - 1]):
                dve.wait_ge(high, n + 1)
                sub(lo, raw, hi).then_inc(low, 1)
            for m in range(XC):
                for half in range(2):
                    b4 = slice(4 * half, 4 * half + 4)
                    dve.wait_ge(kh_done, 2 * m + half + 1)
                    sub(kc_l[m][:, b4, 0:TEXT], bank[2 * m + half][:, 0:448].rearrange("p (b n) -> p b n", b=4),
                        kc_h[m][:, b4, 0:TEXT]).then_inc(kl_done, 1)
            dve.wait_ge(kh_done, 7)
            for m in range(XC):
                ins = sub(kc_l[m][:, :, TEXT:KEYS], spare[0][:, 64 * m:64 * m + 64].rearrange("p (n b) -> p b n", b=B),
                          kc_h[m][:, :, TEXT:KEYS])
            ins.then_inc(kl_done, 1)
            dve.wait_ge(high, Q_SPLIT)
            sub(wq_l[:], w_raw[:, 0, 0:XC, :], wq_h[:]).then_inc(low, 1)
            dve.wait_ge(con_in, 16)
            split_x(0)
            dve.wait_ge(high, V_SPLIT)
            sub(wv_l[:], w_raw[:, 1, :, 0:D], wv_h[:]).then_inc(low, 1)
            dve.wait_ge(high, VIP_SPLIT)
            dve.wait_ge(k_ready, 7)
            sub(wvip_l[:], wvip_raw, wvip_h[:]).then_inc(low, 1)

            dve.wait_ge(box_in, 16)
            steps = 0

            def chained(ins):
                nonlocal steps
                steps += 1
                ins.then_inc(mask_step, 1)
                dve.wait_ge(mask_step, steps)

            for t in range(QT):
                xg, yg = con[:, XG:XG + 1], con[:, YG + t:YG + t + 1]
                o = inside[:, t]
                chained(nc.vector.tensor_scalar(o, box[:, :, :, 0], xg, None, ALU.is_le))
                chained(nc.vector.scalar_tensor_tensor(o, box[:, :, :, 1], yg, o, ALU.is_le, ALU.mult))
                chained(nc.vector.scalar_tensor_tensor(o, box[:, :, :, 2], xg, o, ALU.is_ge, ALU.mult))
                chained(nc.vector.scalar_tensor_tensor(o, box[:, :, :, 3], yg, o, ALU.is_ge, ALU.mult))
                chained(nc.vector.tensor_reduce(some[:, t], o, X, ALU.max))
                nc.vector.tensor_scalar(mask[:, t, :, 0:BOX], some[:, t].unsqueeze(2).to_broadcast([P, B, BOX]),
                                        NEG, None, ALU.mult)
                nc.vector.tensor_scalar(mask[:, t, :, BOX:IP], o, -NEG, NEG, ALU.mult, ALU.add).then_inc(mask_ready, 1)

            dve.wait_ge(high, len(splits))
            sub(wo_l[:], wo_raw, wo_h[:]).then_inc(low, 1)
            dve.wait_ge(mask_ready, QT)

            def low_q(c, part):
                dve.wait_ge(qh_done, 2 * c + part + 1)
                if part == 0:
                    sub(q_l[:, 0:2, :], spare[0][:].rearrange("p (m n) -> p m n", m=2), q_h[:, 0:2, :]).then_inc(ql_done, 1)
                else:
                    sub(q_l[:, 2, :], spare[1][:, 0:S], q_h[:, 2, :]).then_inc(ql_done, 1)

            def read_a(c, n):
                t, g = n // GROUPS, n % GROUPS
                heads = slice(GROUP * g, GROUP * (g + 1))
                dve.wait_ge(a_ready, 2 * GROUPS * c + n + 1)
                if n == 0 and not (isinstance(c, int) and c == 0):
                    dve.wait_ge(shift_ready, c)
                    dve.wait_ge(ipd_done, c)
                s = a_bank[n % 2][:, 0:GROUP * KEYS].rearrange("p (h n) -> p h n", h=GROUP)
                nc.vector.tensor_reduce(negmax[:, t, :, 2 * g:2 * g + 2].rearrange("p a q -> p q a"),
                                        s[:, :, 0:TEXT].rearrange("p (q a) n -> p q a n", a=2), X, ALU.max,
                                        negate=True).then_inc(a_max, 1)
                nc.vector.tensor_tensor(ips[:, t, heads, :], s[:, :, TEXT:KEYS],
                                        mask[:, t, c, :].unsqueeze(1).to_broadcast([P, GROUP, IP]),
                                        ALU.add).then_inc(a_used, 1)

            def image_max(c):
                dve.wait_ge(a_used, 2 * GROUPS * (c + 1))
                nc.vector.tensor_reduce(ipm[:], ips[:], X, ALU.max).then_inc(ipm_done, 1)

            def low_shift(c):
                dve.wait_ge(sh_done, c + 1)
                sub(shift[:, 1], spare[1][0:H, 0:S], shift[:, 0]).then_inc(sl_done, 1)

            def image_sum(c):
                dve.wait_ge(ipe_done, c + 1)
                nc.vector.tensor_reduce(ipz[:], ipe[:], X, ALU.add).then_inc(ipz_done, 1)
                dve.wait_ge(ipz_done, c + 1)
                if not (isinstance(c, int) and c == 0):
                    dve.wait_ge(ipp_done, c)
                nc.vector.reciprocal(ipr[:], ipz[:]).then_inc(ipr_done, 1)

            def low_ip(b, part):
                dve.wait_ge(pih_done, 2 * b + part + 1)
                if part == 0:
                    sub(pip[64:P, 0:2, :], spare[0][0:64, :].rearrange("p (m n) -> p m n", m=2),
                        pip[0:64, 0:2, :]).then_inc(pil_done, 1)
                else:
                    sub(pip[64:P, 2, :], spare[1][0:64, 0:S], pip[0:64, 2, :]).then_inc(pil_done, 1)

            def normalise(b, k, c):
                oz = oz_bank[(k + c) % 2]
                dve.wait_ge(oz_ready, XC * b + c + 1)
                nc.vector.reciprocal(rz[:, (k + c) % 2, :], oz[:, S:2 * S]).then_inc(rz_done, 1)
                dve.wait_ge(rz_done, XC * b + c + 1)
                if c == 0 and not (isinstance(b, int) and b == 0):
                    dve.wait_ge(on_done, XC * b)
                nc.vector.tensor_tensor(ot[:, c, :], oz[:, 0:S], rz[:, (k + c) % 2, :], ALU.mult).then_inc(ot_done, 1)

            def last_chunk_out(b):
                dve.wait_ge(onh_done, XC * (b + 1))
                if not (isinstance(b, int) and b == 0):
                    dve.wait_ge(out_ready, QT * b)
                nc.vector.scalar_tensor_tensor(on_l[:, 2, :], on_h[:, 2, :], con[:, NEG_SECOND:NEG_SECOND + 1],
                                               on[:, 2, :], ALU.mult, ALU.add).then_inc(onl_done, 1)

            def add_residual(b, t):
                dve.wait_ge(out_ready, QT * b + t + 1)
                if t == 0:
                    dve.wait_ge(xb_done, b + 1)
                    if not (isinstance(b, int) and b == 0):
                        dve.wait_ge(y_stored, 16 * b)
                nc.vector.tensor_tensor(y[:, t, :], spare[1 - t][:, 0:D], xb[:, t, :], ALU.add).then_inc(y_done, 1)

            def step(b, k, first=False, last=False):
                c = b + 1
                reads = [] if last else list(range(2 * GROUPS))

                def some_a(n):
                    for _ in range(n):
                        if reads:
                            read_a(c, reads.pop(0))

                if not last:
                    low_q(c, 0)
                    low_q(c, 1)
                low_ip(b, 0)
                low_ip(b, 1)
                if not first:
                    add_residual(b - 1, 0)
                    add_residual(b - 1, 1)
                if not last:
                    split_x(c + 1)
                some_a(2)
                normalise(b, k, 0)
                some_a(4)
                normalise(b, k, 1)
                some_a(4)
                if not last:
                    image_max(c)
                    low_shift(c)
                normalise(b, k, 2)
                if not last:
                    image_sum(c)
                last_chunk_out(b)

            low_q(0, 0)
            low_q(0, 1)
            split_x(1)
            for n in range(2 * GROUPS):
                read_a(0, n)
            image_max(0)
            low_shift(0)
            image_sum(0)
            step(0, 0, first=True)
            with dve.Fori(0, (B - 2) // 2) as i:
                step(2 * i + 1, 1)
                step(2 * i + 2, 0)
            step(B - 1, 1, last=True)
            add_residual(B - 1, 0)
            add_residual(B - 1, 1)

        @block.gpsimd
        def _(pool):
            sub = lambda o, a, b: nc.gpsimd.tensor_tensor(o, a, b, ALU.subtract)
            for tile in (v[0], v[1], ipp, ks[0]):
                nc.gpsimd.memset(tile[:].bitcast(F32) if tile is ks[0] else tile[:], 0.0).then_inc(zeroed, 1)
            pool.wait_ge(con_in, 16)

            def ones(k):
                pool.wait_ge(zeroed, k + 4)
                for ab in range(2):
                    nc.gpsimd.tensor_copy(
                        ks[k][STACK:STACK + SHIFT, :, ab, :],
                        con[STACK:STACK + SHIFT, SHIFT_ROWS + ab:SHIFT_ROWS + ab + 1].unsqueeze(2)
                        .to_broadcast([SHIFT, PAIRS, KEYS])).then_inc(ones_set, 1)
                    pool.wait_ge(ones_set, 2 * k + ab + 1)

            ones(0)

            def split_x(c):
                pool.wait_ge(xh_done, c + 1)
                sub(x_l[:, 0:2, :], x_raw[:, 0:2, :], x_h[:, 0:2, :]).then_inc(xl_done, 1)

            def image_values(c):
                pool.wait_ge(vr_in, 32)
                if not (isinstance(c, int) and c == 0):
                    pool.wait_ge(vip_done, c)
                nc.gpsimd.tensor_tensor(vm[:], vr[:, c], con[:, BLOCK:BLOCK + DP], ALU.mult).then_inc(vm_done, 1)
                if not (isinstance(c, int) and c == 0):
                    pool.wait_ge(oip_ready, 2 * c)
                pool.wait_ge(vm_done, c + 1)
                nc.gpsimd.tensor_tensor(vip_h[:], vm[:], con[:, BLOCK:BLOCK + DP], ALU.mult).then_inc(viph_done, 1)
                pool.wait_ge(viph_done, c + 1)
                sub(vip_l[:], vm[:], vip_h[:]).then_inc(vip_done, 1)

            def image_shift(c):
                pool.wait_ge(ipm_done, c + 1)
                if not (isinstance(c, int) and c == 0):
                    pool.wait_ge(ipe_done, c)
                nc.gpsimd.tensor_tensor(ipd[:], ips[:], ipm[:].unsqueeze(3).to_broadcast([P, QT, H, IP]),
                                        ALU.subtract).then_inc(ipd_done, 1)

            def image_norm(c):
                pool.wait_ge(ipr_done, c + 1)
                if not (isinstance(c, int) and c == 0):
                    pool.wait_ge(ipt_ready, 2 * c)
                nc.gpsimd.tensor_tensor(ipp[:, :, 0:H, :], ipe[:], ipr[:].unsqueeze(3).to_broadcast([P, QT, H, IP]),
                                        ALU.mult).then_inc(ipp_done, 1)

            def residual(b):
                pool.wait_ge(xres_in, 16 * (b + 1))
                if not (isinstance(b, int) and b == 0):
                    pool.wait_ge(y_done, QT * b)
                else:
                    pool.wait_ge(bias_in, 16)
                nc.gpsimd.tensor_tensor(xb[:], x_res[:], bias[:].unsqueeze(1).to_broadcast([P, QT, D]),
                                        ALU.add).then_inc(xb_done, 1)

            def output(b, c):
                pool.wait_ge(ot_done, XC * b + c + 1)
                pool.wait_ge(oi_done, 2 * b + 1 + c // 2)
                if c == 0 and not (isinstance(b, int) and b == 0):
                    pool.wait_ge(onl_done, XC * b)
                nc.gpsimd.tensor_tensor(on[:, c, :], ot[:, c, :], oi[:, c, :], ALU.add).then_inc(on_done, 1)
                if c < 2:
                    pool.wait_ge(onh_done, XC * b + c + 1)
                    sub(on_l[:, c, :], on[:, c, :], on_h[:, c, :]).then_inc(onl_done, 1)

            def step(b, k, first=False, last=False):
                c = b + 1
                if not last:
                    split_x(c + 1)
                residual(b)
                output(b, 0)
                output(b, 1)
                if not last:
                    image_values(c)
                    image_shift(c)
                output(b, 2)
                if not last:
                    image_norm(c)

            split_x(0)
            pool.wait_ge(vipn_ready, 1)
            nc.gpsimd.memset(ks[1][:].bitcast(F32), 0.0).then_inc(zeroed, 1)
            ones(1)
            image_values(0)
            split_x(1)
            image_shift(0)
            image_norm(0)
            step(0, 0, first=True)
            with pool.Fori(0, (B - 2) // 2) as i:
                step(2 * i + 1, 1)
                step(2 * i + 2, 0)
            step(B - 1, 1, last=True)


def kernel(x, ctx_2048, fside_Bx4x4_0, L0_xattn_w_q, L0_xattn_w_k, L0_xattn_w_v, L0_xattn_w_k_ip,
           L0_xattn_w_v_ip, L0_xattn_w_out, L0_xattn_b_out):
    import numpy as np
    import concourse.bacc as bacc
    from concourse.bass_utils import run_bass_kernel_spmd

    x, ctx_all, box = (np.ascontiguousarray(a) for a in (x, ctx_2048, fside_Bx4x4_0))
    wq, wk, wv, wk_ip, wv_ip, w_out, b_out = (np.ascontiguousarray(a) for a in (
        L0_xattn_w_q, L0_xattn_w_k, L0_xattn_w_v, L0_xattn_w_k_ip, L0_xattn_w_v_ip, L0_xattn_w_out, L0_xattn_b_out))

    def by_chunk(rows):
        return np.ascontiguousarray(rows.reshape(-1, P, rows.shape[1]).transpose(1, 0, 2))

    def padded(w):
        return np.pad(w, ((0, 0), (0, DP - D)))

    rows = np.r_[0:D, 2 * P:D]
    out_rows = np.r_[0:2 * P, np.concatenate([np.r_[h * DH:(h + 1) * DH, h * DH:(h + 1) * DH] for h in range(16, H)])]
    xT = x.transpose(0, 2, 1)[:, rows, :].reshape(B, XC, P, S).transpose(0, 2, 1, 3)
    arrays = {
        "xT": np.concatenate([xT, xT[:1]]),
        "x": x,
        "ctxT": by_chunk(ctx_all[:, :TEXT].reshape(B * TEXT, C).T),
        "ctx_ipT": by_chunk(np.tile(ctx_all[:, TEXT:].transpose(2, 1, 0).reshape(C, IP * B), (1, 2))),
        "bbox": box.reshape(B * BOX * 4),
        "wq": by_chunk(padded(wq)[rows]),
        "wk": by_chunk(padded(wk)),
        "wv": by_chunk(wv),
        "wk_ip": by_chunk(padded(wk_ip)),
        "wv_ip": by_chunk(wv_ip[:, out_rows]),
        "w_out": by_chunk(w_out[out_rows]),
        "b_out": b_out,
        "consts": constants(),
    }
    nc = bacc.Bacc("TRN2", target_bir_lowering=False, num_devices=1)
    args = []
    for name, a in arrays.items():
        arrays[name] = a = np.ascontiguousarray(a)
        args.append(nc.dram_tensor(name, a.shape, mybir.dt.from_np(a.dtype), kind="ExternalInput").ap())
    args.append(nc.dram_tensor("out", (B, S, D), F32, kind="ExternalOutput").ap())
    build(nc, *args)
    r = run_bass_kernel_spmd(nc, [arrays], core_ids=[0])
    return r.results[0]["out"]
```

```python
from contextlib import ExitStack

import concourse.bass as bass
from concourse import mybir

F32 = mybir.dt.float32
F32R = mybir.dt.float32r
ALU = mybir.AluOpType
ACT = mybir.ActivationFunctionType
X = mybir.AxisListType.X

P = 128
B, S, D, C = 8, 256, 320, 512
H, DH = 20, 16
TEXT, IP = 112, 8
KEYS = TEXT + IP
BOX = IP // 2
GRID = 16
PAIRS = H // 2
QT = S // P
CC = C // P
XC = 3
DP = XC * P
GROUP = 4
GROUPS = H // GROUP
HPC = P // DH
SCALE = float(DH) ** -0.5
NEG = -10000.0 / SCALE
STACK = 3 * 32
SHIFT = 4

IDENT = 0
XG = IDENT + P
YG = XG + 1
NEG_SECOND = YG + QT
NEG_LOWER = NEG_SECOND + 1
SHIFT_ROWS = NEG_LOWER + 1
SUM_COLS = SHIFT_ROWS + 2
BLOCK = SUM_COLS + 3 * 32
CONSTS = BLOCK + DP


def constants():
    import numpy as np

    c = np.zeros((P, CONSTS), np.float32)
    p = np.arange(P)
    c[:, IDENT:IDENT + P] = np.eye(P)
    lin = np.linspace(0.0, 1.0, GRID, dtype=np.float32)
    c[:, XG] = lin[p % GRID]
    for t in range(QT):
        c[:, YG + t] = lin[(t * P + p) // GRID]
    c[:, NEG_SECOND] = -1.0 * (p % 32 >= DH)
    c[:, NEG_LOWER] = -1.0 * (p >= 64)
    for r in range(SHIFT):
        c[STACK + r, SHIFT_ROWS + r % 2] = 1.0
    c[:, SUM_COLS:SUM_COLS + DH] = 1.0
    c[:, SUM_COLS + 32 + DH:SUM_COLS + 64] = 1.0
    c[:, SUM_COLS + 64:SUM_COLS + 96] = 1.0
    head = p % (HPC * IP) // IP
    for j in range(XC):
        d = np.arange(P)
        own = d // DH if j < 2 else d // 32
        c[:, BLOCK + j * P:BLOCK + (j + 1) * P] = head[:, None] == own[None, :]
    return c


def build(nc, xT, x, ctxT, ctx_ipT, bbox, wq, wk, wv, wk_ip, wv_ip, w_out, b_out, consts, out):
    ctx = ExitStack()
    with ctx:
        def sb(name, shape, dt=F32):
            return ctx.enter_context(nc.sbuf_tensor(name, shape, dt))

        def sem(name):
            return ctx.enter_context(nc.semaphore(name))

        k_dram = nc.dram_tensor("k_dram", (2, PAIRS, 2, DH, B, KEYS), F32, kind="Internal").ap()
        vip_dram = nc.dram_tensor("vip_dram", (HPC, IP, B, DP), F32, kind="Internal").ap()
        q_dram = nc.dram_tensor("q_dram", (2, DP // 32, 32, S), F32, kind="Internal").ap()

        shift_dram = nc.dram_tensor("shift_dram", (2, 2, PAIRS, S), F32, kind="Internal").ap()

        con = sb("con", [P, CONSTS])
        ident = con[:, IDENT:IDENT + P]
        raw = sb("raw", [P, PAIRS * 2 * S + B * D])
        w_raw = raw[:, 0:2 * CC * DP].rearrange("p (s j n) -> p s j n", s=2, j=CC)
        ctx_raw = raw[:, 2 * CC * DP:2 * CC * DP + CC * B * TEXT].rearrange("p (j n) -> p j n", j=CC)
        probs = raw[0:TEXT, 0:PAIRS * 2 * S].rearrange("p (a n) -> p a n", a=PAIRS)
        v_all = raw[0:TEXT, PAIRS * 2 * S:].rearrange("p (b h d) -> p b h d", b=B, h=H)
        ctx_hl = sb("ctx_hl", [P, 2, CC * B * TEXT], F32R)
        ctx_h, ctx_l = (ctx_hl[:, n].rearrange("p (j n) -> p j n", j=CC) for n in range(2))
        vr = ctx_hl[:, 0, 0:B * DP].bitcast(F32).rearrange("p (b n) -> p b n", b=B)
        cip_raw = sb("cip_raw", [P, CC, P])
        cip_h, cip_l = (sb(n, [P, CC, P], F32R) for n in ("cip_h", "cip_l"))
        key_w = sb("key_w", [P, 4, CC * DP], F32R)
        wk_h, wk_l, wkip_h, wkip_l = (key_w[:, n].rearrange("p (j n) -> p j n", j=CC) for n in range(4))
        key_w_flat = key_w[:].rearrange("p s n -> p (s n)")
        wq_h, wq_l = (sb(n, [P, XC, DP], F32R) for n in ("wq_h", "wq_l"))
        wv_h, wv_l = (sb(n, [P, CC, D], F32R) for n in ("wv_h", "wv_l"))
        wo_h, wo_l = (sb(n, [P, XC, D], F32R) for n in ("wo_h", "wo_l"))
        late = sb("late", [P, 3 * XC * S + 2 * QT * D + 2 * S])
        ot, oi, on = (late[:, n * XC * S:(n + 1) * XC * S].rearrange("p (c n) -> p c n", c=XC) for n in range(3))
        at_x = 3 * XC * S
        x_res, y = (late[:, at_x + n * QT * D:at_x + (n + 1) * QT * D].rearrange("p (t n) -> p t n", t=QT)
                    for n in range(2))
        rz = late[:, at_x + 2 * QT * D:].rearrange("p (k n) -> p k n", k=2)
        kc_more = sb("kc_more", [P, 2, B * KEYS])
        kc = [late[:, n * B * KEYS:(n + 1) * B * KEYS] for n in range(4)] + [kc_more[:, n] for n in range(2)]
        kc = [t.bitcast(F32R).rearrange("p (b n) -> p b n", b=B) for t in kc]
        kc_h, kc_l = kc[0:XC], kc[XC:]
        box = sb("box", [P, B, BOX, 4])
        inside = sb("inside", [P, QT, B, BOX])
        some = sb("some", [P, QT, B])
        mask = sb("mask", [P, QT, B, IP])
        bias = sb("bias", [P, D])

        x_raw = sb("x_raw", [P, XC, S])
        x_h, x_l = (sb(n, [P, XC, S], F32R) for n in ("x_h", "x_l"))
        q_h, q_l = (sb(n, [P, XC, S], F32R) for n in ("q_h", "q_l"))
        qs = [sb("qs0", [P, PAIRS, S], F32R),
              key_w_flat[:, 0:PAIRS * S].rearrange("p (a n) -> p a n", a=PAIRS)]
        ks = [sb("ks0", [P, PAIRS, 2, KEYS], F32R),
              key_w_flat[:, 2 * CC * DP:2 * CC * DP + PAIRS * 2 * KEYS].rearrange("p (a s n) -> p a s n", a=PAIRS, s=2)]
        v = [sb(f"v{k}", [TEXT, H, 32]) for k in range(2)]
        negmax = sb("negmax", [P, QT, 2, PAIRS])
        shift = sb("shift", [H, 2, S], F32R)
        ips = sb("ips", [P, QT, H, IP])
        ipd = sb("ipd", [P, QT, H, IP])
        ipe = sb("ipe", [P, QT, H, IP])
        ipm = sb("ipm", [P, QT, H])
        ipz = sb("ipz", [P, QT, H])
        ipr = sb("ipr", [P, QT, H])
        ipp = sb("ipp", [P, QT, XC * HPC, IP])
        pip = sb("pip", [P, XC, S], F32R)
        vipn = sb("vipn", [B * IP, DP])
        vm = sb("vm", [P, DP])
        vip_h, vip_l = (sb(n, [P, DP], F32R) for n in ("vip_h", "vip_l"))
        on_h, on_l = (ctx_hl[:, 1, n * XC * S:(n + 1) * XC * S].rearrange("p (c n) -> p c n", c=XC) for n in range(2))
        log_z = sb("log_z", [P, 2, S])
        zr = sb("zr", [P, S])
        xb = sb("xb", [P, QT, D])

        bank = [ctx.enter_context(nc.psum_tensor(f"bank{i}", [P, 512], F32)) for i in range(8)]
        a_bank = bank[0:2]
        b_bank = bank[2:4]
        oz_bank = bank[4:6]
        spare = bank[6:8]
        v_bank = bank[2:6]

        wk_ctx_in = [sem(f"wk_ctx_in{j}") for j in range(CC)]
        kip_in, vip_w_in, wq_in, wv_in, wo_in = (sem(n) for n in ("kip_in", "vip_w_in", "wq_in", "wv_in", "wo_in"))
        con_in, box_in, bias_in = (sem(n) for n in ("con_in", "box_in", "bias_in"))
        x_in, xres_in, ks_in, vr_in = (sem(n) for n in ("x_in", "xres_in", "ks_in", "vr_in"))
        high, low = sem("high"), sem("low")
        zeroed, ones_set, mask_ready, mask_step = (sem(n) for n in ("zeroed", "ones_set", "mask_ready", "mask_step"))
        k_ready, kh_done, kl_done, k_stored = (sem(n) for n in ("k_ready", "kh_done", "kl_done", "k_stored"))
        vipn_ready, vipn_done, vipn_stored = (sem(n) for n in ("vipn_ready", "vipn_done", "vipn_stored"))
        xh_done, xl_done = sem("xh_done"), sem("xl_done")
        q_ready, qh_done, ql_done, q_stored, qs_in = (
            sem(n) for n in ("q_ready", "qh_done", "ql_done", "q_stored", "qs_in"))
        va_ready, va_done, v_done = sem("va_ready"), sem("va_done"), sem("v_done")
        a_ready, a_max, a_used = sem("a_ready"), sem("a_max"), sem("a_used")
        shift_ready, sh_done, sl_done, shift_in = (sem(n) for n in ("shift_ready", "sh_done", "sl_done", "shift_in"))
        shift_stored = sem("shift_stored")
        ipm_done, ipd_done, ipe_done, ipz_done, ipr_done, ipp_done = (
            sem(n) for n in ("ipm_done", "ipd_done", "ipe_done", "ipz_done", "ipr_done", "ipp_done"))
        ipt_ready, pih_done, pil_done = sem("ipt_ready"), sem("pih_done"), sem("pil_done")
        vm_done, viph_done, vip_done = sem("vm_done"), sem("viph_done"), sem("vip_done")
        oip_ready, oi_done = sem("oip_ready"), sem("oi_done")
        b_ready, p_done, oz_ready = sem("b_ready"), sem("p_done"), sem("oz_ready")
        log_done, seed_done, zr_done, rz_done = (sem(n) for n in ("log_done", "seed_done", "zr_done", "rz_done"))
        ot_done, on_done, onh_done, onl_done = (sem(n) for n in ("ot_done", "on_done", "onh_done", "onl_done"))
        out_ready, xb_done, y_done, y_stored = (sem(n) for n in ("out_ready", "xb_done", "y_done", "y_stored"))

        splits = []
        for j in range(CC):
            splits.append((wk_ctx_in[j], 32, wk_h[:, j, :], wk_l[:, j, :], w_raw[:, 0, j, :]))
            splits.append((wk_ctx_in[j], 32, ctx_h[:, j, :], ctx_l[:, j, :], ctx_raw[:, j, :]))
        splits.append((kip_in, 32, cip_h[:], cip_l[:], cip_raw[:]))
        splits.append((kip_in, 32, wkip_h[:], wkip_l[:], w_raw[:, 1]))
        K_SPLIT = len(splits)
        splits.append((wq_in, 16, wq_h[:], wq_l[:], w_raw[:, 0, 0:XC, :]))
        Q_SPLIT = len(splits)
        splits.append((wv_in, 16, wv_h[:], wv_l[:], w_raw[:, 1, :, 0:D]))
        V_SPLIT = len(splits)
        splits.append((vip_w_in, 16, wkip_h[:], wkip_l[:], ctx_raw[:, :, 0:DP]))
        VIP_SPLIT = len(splits)
        splits.append((wo_in, 16, wo_h[:], wo_l[:], ctx_raw[:, 0:XC, DP:DP + D]))
        wo_raw = ctx_raw[:, 0:XC, DP:DP + D]
        wvip_h, wvip_l, wvip_raw = wkip_h, wkip_l, ctx_raw[:, :, 0:DP]

        def chunk_heads(c):
            if c < 2:
                return [(j, 4 * c + j, ab, ab) for ab in range(2) for j in range(4)]
            return [(j, 8 + j // 2, j % 2, 2) for j in range(4)]

        def exists(b):
            return not isinstance(b, int) or 0 <= b < B

        def every_step(engine, step):
            step(0, 0)
            with engine.Fori(0, (B - 4) // 2) as i:
                step(2 * i + 1, 1)
                step(2 * i + 2, 0)
            for b in range(B - 3, B):
                step(b, b % 2)

        block = ctx.enter_context(nc.Block())

        @block.sync
        def _(sp):
            for j in range(CC):
                sp.dma_start(w_raw[:, 0, j, :], wk[:, j, :]).then_inc(wk_ctx_in[j], 16)
                sp.dma_start(ctx_raw[:, j, :], ctxT[:, j, :]).then_inc(wk_ctx_in[j], 16)
            sp.dma_start(cip_raw[:], ctx_ipT).then_inc(kip_in, 16)
            sp.dma_start(w_raw[:, 1], wk_ip).then_inc(kip_in, 16)
            sp.dma_start(con[:], consts).then_inc(con_in, 16)
            sp.dma_start(x_raw[:], xT[0]).then_inc(x_in, 16)
            sp.dma_start(box[:].rearrange("p b m c -> p (b m c)"), bbox.partition_broadcast(P)).then_inc(box_in, 16)
            sp.dma_start(bias[:], b_out.partition_broadcast(P)).then_inc(bias_in, 16)
            sp.wait_ge(high, 2 * CC)
            sp.wait_ge(low, 2 * CC)
            sp.dma_start(w_raw[:, 0, 0:XC, :], wq).then_inc(wq_in, 16)
            sp.dma_start(ctx_raw[:, :, 0:DP], wv_ip).then_inc(vip_w_in, 16)
            sp.dma_start(wo_raw, w_out).then_inc(wo_in, 16)
            sp.wait_ge(high, K_SPLIT)
            sp.wait_ge(low, K_SPLIT)
            sp.dma_start(w_raw[:, 1, :, 0:D], wv).then_inc(wv_in, 16)

            def keys(c, k, blk):
                for ab in range(2):
                    r = 32 * blk + DH * ab
                    sp.dma_start(ks[k][r:r + DH, :, ab, :].bitcast(F32),
                                 k_dram[blk % 2, :, ab, :, c, :].rearrange("p d n -> d p n")).then_inc(ks_in, 16)

            def store_queries(c):
                if not (isinstance(c, int) and c == 0):
                    sp.wait_ge(qs_in, 16 * 3 * c)
                for part, (done, tile) in enumerate(((qh_done, q_h), (ql_done, q_l))):
                    sp.wait_ge(done, 2 * (c + 1))
                    sp.dma_start(q_dram[part].rearrange("(m j) r n -> (j r) m n", m=XC),
                                 tile[:].bitcast(F32)).then_inc(q_stored, 16)

            def queries(c, k):
                sp.wait_ge(q_stored, 16 * 2 * (c + 1))
                for blk, part in enumerate((0, 0, 1)):
                    sp.dma_start(qs[k][32 * blk:32 * blk + 32, :, :].bitcast(F32),
                                 q_dram[part, 0:PAIRS].rearrange("a r n -> r a n")).then_inc(qs_in, 16)

            def store_shifts(c):
                if not (isinstance(c, int) and c == 0):
                    sp.wait_ge(shift_in, 16 * c)
                sp.wait_ge(sh_done, c + 1)
                sp.wait_ge(sl_done, c + 1)
                sp.dma_start(shift_dram.rearrange("s a p n -> (a p) s n"),
                             shift[:].bitcast(F32)).then_inc(shift_stored, 16)

            def shifts(c, k):
                sp.wait_ge(shift_stored, 16 * (c + 1))
                sp.dma_start(qs[k][STACK:STACK + SHIFT, :, :].bitcast(F32),
                             shift_dram.rearrange("s a p n -> (s a) p n")).then_inc(shift_in, 16)

            def store(b):
                sp.wait_ge(y_done, QT * (b + 1))
                sp.dma_start(out[b].rearrange("(t p) d -> p t d", p=P), y[:]).then_inc(y_stored, 16)

            def residual(b):
                if not (isinstance(b, int) and b == 0):
                    sp.wait_ge(xb_done, b)
                sp.dma_start(x_res[:], x[b].rearrange("(t p) d -> p t d", p=P)).then_inc(xres_in, 16)

            def load_x(c):
                sp.wait_ge(xl_done, 2 * c)
                sp.wait_ge(xh_done, c)
                sp.dma_start(x_raw[:], xT[c]).then_inc(x_in, 16)

            def step(b, k):
                if exists(b + 3):
                    load_x(b + 3)
                residual(b)
                if exists(b + 2):
                    store_queries(b + 2)
                if exists(b + 2):
                    sp.wait_ge(b_ready, PAIRS * (b + 1))
                    keys(b + 2, k, 0)
                if exists(b + 1):
                    store_shifts(b + 1)
                if exists(b + 2):
                    queries(b + 2, k)
                    keys(b + 2, k, 1)
                if exists(b + 1):
                    shifts(b + 1, 1 - k)
                if exists(b + 2):
                    keys(b + 2, k, 2)
                if exists(b - 1):
                    store(b - 1)

            load_x(1)
            sp.wait_ge(kh_done, 7)
            sp.wait_ge(kl_done, 7)
            for part, kc_part in enumerate((kc_h, kc_l)):
                rows = k_dram[part].rearrange("p a d b n -> (p a d) (b n)")
                for m in range(XC):
                    n = min(P, D - m * P)
                    sp.dma_start(rows[m * P:m * P + n, :],
                                 kc_part[m][0:n].bitcast(F32).rearrange("p b n -> p (b n)")).then_inc(k_stored, 16)
            store_queries(0)
            load_x(2)
            sp.wait_ge(zeroed, 4)
            sp.wait_ge(k_stored, 16 * 2 * XC)
            for blk in range(3):
                keys(0, 0, blk)
            queries(0, 0)
            sp.wait_ge(vipn_done, 1)
            sp.dma_start(vip_dram.rearrange("h k b n -> (k b) h n"),
                         vipn[:].unsqueeze(1).to_broadcast([B * IP, HPC, DP])).then_inc(vipn_stored, 16)
            store_queries(1)
            sp.wait_ge(zeroed, 5)
            for blk in range(3):
                keys(1, 1, blk)
            queries(1, 1)
            store_shifts(0)
            shifts(0, 0)
            sp.wait_ge(va_ready, B)
            sp.wait_ge(vipn_stored, 16)
            for half in range(2):
                sp.dma_start(vr[64 * half:64 * half + 64],
                             vip_dram.rearrange("h k b n -> (h k) b n")).then_inc(vr_in, 16)
            every_step(sp, step)
            store(B - 1)
            sp.wait_ge(y_stored, 16 * B)

        @block.tensor
        def _(pe):
            def three(out_ap, products, start=True, stop=True):
                for n, (lhsT, rhs) in enumerate(products):
                    mm = pe.matmul(out_ap, lhsT, rhs, start=start and n == 0, stop=stop and n == len(products) - 1)
                return mm

            for j in range(CC):
                pe.wait_ge(high, 2 * j + 2)
                pe.wait_ge(low, 2 * j + 2)
                for m in range(XC):
                    w_hi, w_lo = (w[:, j, m * P:(m + 1) * P] for w in (wk_h, wk_l))
                    for half in range(2):
                        n = slice(half * 448, half * 448 + 448)
                        mm = three(bank[2 * m + half][:, 0:448],
                                   [(w_hi, ctx_h[:, j, n]), (w_hi, ctx_l[:, j, n]), (w_lo, ctx_h[:, j, n])],
                                   start=j == 0, stop=j == CC - 1)
                        if j == CC - 1:
                            mm.then_inc(k_ready, 1)
            pe.wait_ge(high, K_SPLIT)
            pe.wait_ge(low, K_SPLIT)
            for m in range(XC):
                mm = three(spare[0][:, 64 * m:64 * m + 64],
                           [(w[:, j, m * P:(m + 1) * P], t[:, j, 0:B * IP]) for j in range(CC)
                            for w, t in ((wkip_h, cip_h), (wkip_h, cip_l), (wkip_l, cip_h))])
            mm.then_inc(k_ready, 1)
            def image_values():
                pe.wait_ge(high, VIP_SPLIT)
                pe.wait_ge(low, VIP_SPLIT)
                three(spare[1][:, 0:DP],
                      [(t[:, j, :], w[:, j, :]) for j in range(CC)
                       for t, w in ((cip_h, wvip_h), (cip_h, wvip_l), (cip_l, wvip_h))]).then_inc(vipn_ready, 1)

            def project_q(c):
                pe.wait_ge(xh_done, c + 1)
                pe.wait_ge(xl_done, 2 * (c + 1))
                for m in range(XC):
                    cols = slice(m * P, (m + 1) * P)
                    prods = [(w[:, j, cols], t[:, j, :]) for j in range(2)
                             for w, t in ((wq_h, x_h), (wq_h, x_l), (wq_l, x_h))]
                    prods += [(wq_h[:, 2, cols], x_l[:, 2, :]), (wq_l[:, 2, cols], x_l[:, 2, :])]
                    mm = three(spare[m // 2][:, S * (m % 2):S * (m % 2) + S], prods)
                    if m:
                        mm.then_inc(q_ready, 1)

            def project_v(b):
                if b >= 4:
                    pe.wait_ge(va_done, b - 3)
                n = slice(b * TEXT, (b + 1) * TEXT)
                three(v_bank[b % 4][0:TEXT, 0:D],
                      [(t[:, j, n], w[:, j, :]) for j in range(CC)
                       for t, w in ((ctx_h, wv_h), (ctx_h, wv_l), (ctx_l, wv_h))]).then_inc(va_ready, 1)

            def score_a(c, k, n):
                if n == 0:
                    pe.wait_ge(qs_in, 16 * 3 * (c + 1))
                    pe.wait_ge(ks_in, 16 * 6 * (c + 1))
                t, g = n // GROUPS, n % GROUPS
                if n >= 2 or not (isinstance(c, int) and c == 0):
                    pe.wait_ge(a_used, 2 * GROUPS * c + n - 1)
                for p in range(2):
                    mm = pe.matmul(a_bank[n % 2][:, 2 * KEYS * p:2 * KEYS * (p + 1)],
                                   qs[k][0:STACK, 2 * g + p, t * P:(t + 1) * P],
                                   ks[k][0:STACK, 2 * g + p, :, :].rearrange("p a n -> p (a n)"),
                                   start=True, stop=True)
                mm.then_inc(a_ready, 1)

            def transpose_max(c):
                pe.wait_ge(a_max, 2 * GROUPS * (c + 1))
                for t in range(QT):
                    mm = pe.transpose(spare[1][0:H, t * P:(t + 1) * P], negmax[:, t].rearrange("p a n -> p (a n)"), ident)
                mm.then_inc(shift_ready, 1)

            def score_b(b, k, p):
                if p == 0:
                    pe.wait_ge(shift_in, 16 * (b + 1))
                if p >= 2 or not (isinstance(b, int) and b == 0):
                    pe.wait_ge(p_done, PAIRS * b + p - 1)
                for ab in range(2):
                    mm = pe.matmul(b_bank[p % 2][0:TEXT, S * ab:S * ab + S],
                                   ks[k][0:STACK + SHIFT, p, ab, 0:TEXT],
                                   qs[k][0:STACK + SHIFT, p, :], start=True, stop=True)
                mm.then_inc(b_ready, 1)

            def transpose_ip(b, k, part):
                if part == 0:
                    pe.wait_ge(con_in, 16)
                    pe.wait_ge(ipp_done, b + 1)
                for c in (2,) if part == 0 else (0, 1):
                    for t in range(QT):
                        at = S * (c % 2) + t * P
                        mm = pe.transpose(oz_bank[(k + part) % 2][0:HPC * IP, at:at + P],
                                          ipp[:, t, HPC * c:HPC * (c + 1), :].rearrange("p h n -> p (h n)"), ident)
                mm.then_inc(ipt_ready, 1)

            def image_out(b, part):
                if part == 0:
                    pe.wait_ge(pih_done, 2 * (b + 1))
                    pe.wait_ge(pil_done, 2 * (b + 1))
                    pe.wait_ge(vip_done, b + 1)
                for c in (0, 1) if part == 0 else (2,):
                    cols = slice(c * P, (c + 1) * P)
                    mm = three(spare[1 - part][:, S * (c % 2):S * (c % 2) + S],
                               [(w[:, cols], pip[:, c, :]) for w in (vip_h, vip_l)])
                mm.then_inc(oip_ready, 1)

            def text_out(b, k, c, what):
                heads = chunk_heads(c)
                turn = (k + c) % 2
                if what == 0:
                    pe.wait_ge(p_done, PAIRS * b + (4, 8, 10)[c])
                    if c == 0:
                        pe.wait_ge(v_done, b + 1)
                    if c < 2:
                        pe.wait_ge(pil_done, 2 * b + c + 1)
                    if c == 2 or not (isinstance(b, int) and b == 0):
                        pe.wait_ge(ot_done, XC * b + c - 1)
                for n, (j, p, ab, cols) in enumerate(heads):
                    w = (v[k][:, 2 * p + ab, :],
                         con[0:TEXT, SUM_COLS + 32 * cols:SUM_COLS + 32 * cols + 32])[what]
                    mm = pe.matmul(oz_bank[turn][32 * j:32 * j + 32, S * what:S * what + S], w,
                                   probs[:, p, S * ab:S * ab + S],
                                   start=what == 0 and n < 4, stop=n >= len(heads) - 4,
                                   skip_group_check=True)
                if what:
                    mm.then_inc(oz_ready, 1)

            def project_out(b, t, chunks=range(XC)):
                q = slice(t * P, (t + 1) * P)
                for j in chunks:
                    if t == 0:
                        pe.wait_ge(onh_done, XC * b + j + 1)
                        pe.wait_ge(onl_done, XC * b + j + 1)
                    prods = (((on_h, wo_h), (on_h, wo_l), (on_l, wo_h)) if j < XC - 1 else
                             ((on_l, wo_h), (on_l, wo_l)))
                    mm = three(spare[t][:, 0:D], [(o[:, j, q], w[:, j, :]) for o, w in prods],
                               start=j == 0, stop=j == XC - 1)
                if j == XC - 1:
                    mm.then_inc(out_ready, 1)

            def step(b, k):
                c = b + 1
                if exists(b - 1) and exists(b + 2):
                    pe.wait_ge(sl_done, c)
                    pe.wait_ge(oi_done, 2 * b)
                    pe.wait_ge(ot_done, XC * b - 2)
                    project_q(b + 2)
                a = [n for n in range(2 * GROUPS) if exists(c)]

                def more_a(n):
                    for _ in range(n):
                        score_a(c, 1 - k, a.pop(0))

                def both(p):
                    if a:
                        more_a(1)
                    score_b(b, k, p)

                if not exists(b - 1):
                    more_a(2)
                    pe.wait_ge(sl_done, c)
                    project_q(b + 2)
                    transpose_ip(b, k, 0)
                    transpose_ip(b, k, 1)
                    more_a(2)
                    for p in range(4):
                        score_b(b, k, p)
                else:
                    score_b(b, k, 0)
                    pe.wait_ge(ot_done, XC * b)
                    if exists(c):
                        more_a(1)
                    both(1)
                    transpose_ip(b, k, 0)
                    transpose_ip(b, k, 1)
                    both(2)
                    both(3)
                if not exists(c):
                    project_out(b - 1, 0)
                    project_out(b - 1, 1)
                text_out(b, k, 0, 0)
                both(4)
                text_out(b, k, 0, 1)
                both(5)
                if exists(b + 2):
                    pe.wait_ge(ql_done, 2 * (b + 3))
                elif exists(c):
                    pe.wait_ge(y_done, QT * (b - 1))
                    pe.wait_ge(sl_done, c)
                else:
                    pe.wait_ge(y_done, QT * b)
                image_out(b, 0)
                both(6)
                image_out(b, 1)
                both(7)
                both(8)
                both(9)
                if exists(c):
                    pe.wait_ge(oi_done, 2 * b + 1)
                    transpose_max(c)
                if exists(b - 1) and exists(c):
                    pe.wait_ge(oi_done, 2 * b + 2)
                    project_out(b - 1, 0)
                    pe.wait_ge(sl_done, c + 1)
                    project_out(b - 1, 1)
                for chunk in (1, 2):
                    for what in range(2):
                        text_out(b, k, chunk, what)

            pe.wait_ge(high, V_SPLIT)
            pe.wait_ge(low, V_SPLIT)
            pe.wait_ge(kl_done, 6)
            project_v(0)
            project_v(1)
            pe.wait_ge(kl_done, 7)
            project_q(0)
            project_v(2)
            project_v(3)
            pe.wait_ge(ql_done, 2)
            image_values()
            pe.wait_ge(vipn_done, 1)
            project_q(1)
            project_v(4)
            project_v(5)
            for n in range(2 * GROUPS):
                score_a(0, 0, n)
                if n in (1, 3):
                    project_v(6 + n // 2)
            pe.wait_ge(ql_done, 4)
            pe.wait_ge(va_done, B)
            pe.wait_ge(con_in, 16)
            transpose_max(0)
            pe.wait_ge(low, len(splits))
            pe.wait_ge(ones_set, 4)
            every_step(pe, step)
            pe.wait_ge(oi_done, 2 * B)
            for j in range(XC):
                for t in range(QT):
                    project_out(B - 1, t, [j])

        @block.scalar
        def _(act):
            copy = nc.scalar.copy
            nc.scalar.preload_act_table_set("natural_log_exp_and_others")
            def split(n):
                loaded, count, hi, _, raw = splits[n]
                act.wait_ge(loaded, count)
                copy(hi, raw).then_inc(high, 1)

            def split_x(c):
                act.wait_ge(x_in, 16 * (c + 1))
                copy(x_h[:], x_raw[:]).then_inc(xh_done, 1)

            for n in range(K_SPLIT):
                split(n)
            split_x(0)
            split(Q_SPLIT - 1)
            for m in range(XC):
                for half in range(2):
                    act.wait_ge(k_ready, 2 * m + half + 1)
                    copy(kc_h[m][:, 4 * half:4 * half + 4, 0:TEXT],
                         bank[2 * m + half][:, 0:448].rearrange("p (b n) -> p b n", b=4)).then_inc(kh_done, 1)
            split(V_SPLIT - 1)
            act.wait_ge(k_ready, 7)
            for m in range(XC):
                mm = copy(kc_h[m][:, :, TEXT:KEYS],
                          spare[0][:, 64 * m:64 * m + 64].rearrange("p (n b) -> p b n", b=B))
            mm.then_inc(kh_done, 1)
            split(VIP_SPLIT - 1)
            split(VIP_SPLIT)

            def high_q(c, part):
                act.wait_ge(q_ready, 2 * c + part + 1)
                if part == 0 and not (isinstance(c, int) and c == 0):
                    act.wait_ge(q_stored, 32 * c)
                if part == 0:
                    copy(q_h[:, 0:2, :], spare[0][:].rearrange("p (m n) -> p m n", m=2)).then_inc(qh_done, 1)
                else:
                    copy(q_h[:, 2, :], spare[1][:, 0:S]).then_inc(qh_done, 1)

            def values(c, k):
                if not (isinstance(c, int) and c < 2):
                    act.wait_ge(oz_ready, XC * (c - 1))
                src = v_all[:, c]
                copy(v[k][:, 0:16:2, 0:DH], src[:, 0:16:2, :])
                copy(v[k][:, 1:16:2, DH:32], src[:, 1:16:2, :])
                copy(v[k][:, 16:H, 0:DH], src[:, 16:H, :])
                copy(v[k][:, 16:H, DH:32], src[:, 16:H, :]).then_inc(v_done, 1)

            def high_shift(c):
                act.wait_ge(shift_ready, c + 1)
                if not (isinstance(c, int) and c == 0):
                    act.wait_ge(shift_stored, 16 * c)
                copy(shift[:, 0], spare[1][0:H, 0:S]).then_inc(sh_done, 1)

            def image_exp(c):
                act.wait_ge(ipd_done, c + 1)
                if not (isinstance(c, int) and c == 0):
                    act.wait_ge(ipp_done, c)
                nc.scalar.activation(ipe[:], ipd[:], ACT.Exp, scale=SCALE).then_inc(ipe_done, 1)

            def probabilities(b, p):
                act.wait_ge(b_ready, PAIRS * b + p + 1)
                if p in (0, 4, 8) and not (isinstance(b, int) and b == 0):
                    act.wait_ge(oz_ready, XC * (b - 1) + p // 4 + 1)
                nc.scalar.activation(probs[:, p, :], b_bank[p % 2][0:TEXT, :], ACT.Exp,
                                     scale=SCALE).then_inc(p_done, 1)

            def high_ip(b, k, part):
                act.wait_ge(ipt_ready, 2 * b + part + 1)
                if part == 0:
                    if not (isinstance(b, int) and b == 0):
                        act.wait_ge(oip_ready, 2 * b)
                    copy(pip[0:64, 2, :], oz_bank[k][0:64, 0:S]).then_inc(pih_done, 1)
                else:
                    copy(pip[0:64, 0:2, :],
                         oz_bank[1 - k][0:64, :].rearrange("p (m n) -> p m n", m=2)).then_inc(pih_done, 1)

            def image_part(b, part):
                act.wait_ge(oip_ready, 2 * b + part + 1)
                if part == 0:
                    if not (isinstance(b, int) and b == 0):
                        act.wait_ge(on_done, XC * b)
                    copy(oi[:, 0:2, :], spare[1][:].rearrange("p (m n) -> p m n", m=2)).then_inc(oi_done, 1)
                else:
                    copy(oi[:, 2, :], spare[0][:, 0:S]).then_inc(oi_done, 1)

            def high_out(b, c):
                act.wait_ge(on_done, XC * b + c + 1)
                if c == 0 and not (isinstance(b, int) and b == 0):
                    act.wait_ge(out_ready, QT * b)
                copy(on_h[:, c, :], on[:, c, :]).then_inc(onh_done, 1)

            def seed(b, k, c):
                turn = (k + c) % 2
                act.wait_ge(oz_ready, XC * b + c + 1)
                if c == 2 or not (isinstance(b, int) and b == 0):
                    act.wait_ge(ot_done, XC * b + c - 1)
                nc.scalar.activation(log_z[:, turn, :], oz_bank[turn][:, S:2 * S], ACT.Ln).then_inc(log_done, 1)
                act.wait_ge(log_done, XC * b + c + 1)
                nc.scalar.activation(rz[:, turn, :], log_z[:, turn, :], ACT.Exp, scale=-1.0).then_inc(seed_done, 1)

            def step(b, k):
                c = b + 1
                if exists(b + 2):
                    high_q(b + 2, 0)
                    if exists(b - 1):
                        high_out(b - 1, 1)
                    high_q(b + 2, 1)
                if exists(b - 1):
                    probabilities(b, 0)
                if exists(b - 1) and not exists(b + 2):
                    high_out(b - 1, 1)
                if exists(b - 1):
                    probabilities(b, 1)
                high_ip(b, k, 0)
                high_ip(b, k, 1)
                if not exists(b - 1):
                    probabilities(b, 0)
                    probabilities(b, 1)
                if not exists(c):
                    high_out(b - 1, 2)
                probabilities(b, 2)
                probabilities(b, 3)
                if exists(b - 1) and exists(c):
                    high_out(b - 1, 2)
                if exists(b + 3):
                    act.wait_ge(q_ready, 2 * (b + 3))
                    split_x(b + 3)
                probabilities(b, 4)
                if exists(c):
                    values(c, 1 - k)
                probabilities(b, 5)
                seed(b, k, 0)
                probabilities(b, 6)
                image_part(b, 0)
                probabilities(b, 7)
                image_part(b, 1)
                probabilities(b, 8)
                probabilities(b, 9)
                if exists(c):
                    high_shift(c)
                    image_exp(c)
                seed(b, k, 1)
                high_out(b, 0)
                seed(b, k, 2)

            act.wait_ge(high, len(splits))
            act.wait_ge(low, len(splits))

            def copy_v(b):
                act.wait_ge(va_ready, b + 1)
                copy(v_all[:, b], v_bank[b % 4][0:TEXT, 0:D].rearrange("p (h d) -> p h d", h=H)).then_inc(va_done, 1)

            copy_v(0)
            copy_v(1)
            high_q(0, 0)
            high_q(0, 1)
            act.wait_ge(q_ready, 2)
            split_x(1)
            copy_v(2)
            copy_v(3)
            act.wait_ge(vipn_ready, 1)
            copy(vipn[:], spare[1][0:B * IP, 0:DP]).then_inc(vipn_done, 1)
            high_q(1, 0)
            high_q(1, 1)
            act.wait_ge(q_ready, 4)
            split_x(2)
            for b in range(4, B):
                copy_v(b)
            act.wait_ge(va_done, B)
            act.wait_ge(zeroed, 4)
            values(0, 0)
            high_shift(0)
            image_exp(0)
            every_step(act, step)
            high_out(B - 1, 1)
            high_out(B - 1, 2)

        @block.vector
        def _(dve):
            sub = lambda o, a, b: nc.vector.tensor_tensor(o, a, b, ALU.subtract)

            def split_x(c):
                dve.wait_ge(xh_done, c + 1)
                nc.vector.scalar_tensor_tensor(x_l[:, 2, :], x_h[:, 2, :], con[:, NEG_LOWER:NEG_LOWER + 1],
                                               x_raw[:, 2, :], ALU.mult, ALU.add).then_inc(xl_done, 1)

            def split(n):
                _, _, hi, lo, raw = splits[n]
                dve.wait_ge(high, n + 1)
                sub(lo, raw, hi).then_inc(low, 1)

            for n in range(K_SPLIT):
                split(n)
            dve.wait_ge(con_in, 16)
            split_x(0)

            dve.wait_ge(box_in, 16)
            steps = 0

            def chained(ins):
                nonlocal steps
                steps += 1
                ins.then_inc(mask_step, 1)
                dve.wait_ge(mask_step, steps)

            for t in range(QT):
                xg, yg = con[:, XG:XG + 1], con[:, YG + t:YG + t + 1]
                o = inside[:, t]
                chained(nc.vector.tensor_scalar(o, box[:, :, :, 0], xg, None, ALU.is_le))
                chained(nc.vector.scalar_tensor_tensor(o, box[:, :, :, 1], yg, o, ALU.is_le, ALU.mult))
                chained(nc.vector.scalar_tensor_tensor(o, box[:, :, :, 2], xg, o, ALU.is_ge, ALU.mult))
                chained(nc.vector.scalar_tensor_tensor(o, box[:, :, :, 3], yg, o, ALU.is_ge, ALU.mult))
                chained(nc.vector.tensor_reduce(some[:, t], o, X, ALU.max))
                nc.vector.tensor_scalar(mask[:, t, :, 0:BOX], some[:, t].unsqueeze(2).to_broadcast([P, B, BOX]),
                                        NEG, None, ALU.mult)
                nc.vector.tensor_scalar(mask[:, t, :, BOX:IP], o, -NEG, NEG, ALU.mult, ALU.add).then_inc(mask_ready, 1)

            split(Q_SPLIT - 1)
            for m in range(XC):
                for half in range(2):
                    b4 = slice(4 * half, 4 * half + 4)
                    dve.wait_ge(kh_done, 2 * m + half + 1)
                    sub(kc_l[m][:, b4, 0:TEXT], bank[2 * m + half][:, 0:448].rearrange("p (b n) -> p b n", b=4),
                        kc_h[m][:, b4, 0:TEXT]).then_inc(kl_done, 1)
            split(V_SPLIT - 1)
            dve.wait_ge(kh_done, 7)
            for m in range(XC):
                ins = sub(kc_l[m][:, :, TEXT:KEYS], spare[0][:, 64 * m:64 * m + 64].rearrange("p (n b) -> p b n", b=B),
                          kc_h[m][:, :, TEXT:KEYS])
            ins.then_inc(kl_done, 1)
            split(VIP_SPLIT - 1)
            split(VIP_SPLIT)
            dve.wait_ge(mask_ready, QT)

            def low_q(c, part):
                dve.wait_ge(qh_done, 2 * c + part + 1)
                if part == 0:
                    sub(q_l[:, 0:2, :], spare[0][:].rearrange("p (m n) -> p m n", m=2), q_h[:, 0:2, :]).then_inc(ql_done, 1)
                else:
                    sub(q_l[:, 2, :], spare[1][:, 0:S], q_h[:, 2, :]).then_inc(ql_done, 1)

            def read_a(c, n):
                t, g = n // GROUPS, n % GROUPS
                heads = slice(GROUP * g, GROUP * (g + 1))
                dve.wait_ge(a_ready, 2 * GROUPS * c + n + 1)
                if n == 0 and not (isinstance(c, int) and c == 0):
                    dve.wait_ge(shift_ready, c)
                    dve.wait_ge(ipd_done, c)
                s = a_bank[n % 2][:, 0:GROUP * KEYS].rearrange("p (h n) -> p h n", h=GROUP)
                nc.vector.tensor_reduce(negmax[:, t, :, 2 * g:2 * g + 2].rearrange("p a q -> p q a"),
                                        s[:, :, 0:TEXT].rearrange("p (q a) n -> p q a n", a=2), X, ALU.max,
                                        negate=True).then_inc(a_max, 1)
                nc.vector.tensor_tensor(ips[:, t, heads, :], s[:, :, TEXT:KEYS],
                                        mask[:, t, c, :].unsqueeze(1).to_broadcast([P, GROUP, IP]),
                                        ALU.add).then_inc(a_used, 1)

            def image_max(c):
                dve.wait_ge(a_used, 2 * GROUPS * (c + 1))
                nc.vector.tensor_reduce(ipm[:], ips[:], X, ALU.max).then_inc(ipm_done, 1)

            def low_shift(c):
                dve.wait_ge(sh_done, c + 1)
                sub(shift[:, 1], spare[1][0:H, 0:S], shift[:, 0]).then_inc(sl_done, 1)

            def image_sum(c):
                dve.wait_ge(ipe_done, c + 1)
                nc.vector.tensor_reduce(ipz[:], ipe[:], X, ALU.add).then_inc(ipz_done, 1)
                dve.wait_ge(ipz_done, c + 1)
                if not (isinstance(c, int) and c == 0):
                    dve.wait_ge(ipp_done, c)
                nc.vector.reciprocal(ipr[:], ipz[:]).then_inc(ipr_done, 1)

            def low_ip(b, k, part):
                dve.wait_ge(pih_done, 2 * b + part + 1)
                if part == 0:
                    sub(pip[64:P, 2, :], oz_bank[k][0:64, 0:S], pip[0:64, 2, :]).then_inc(pil_done, 1)
                else:
                    sub(pip[64:P, 0:2, :], oz_bank[1 - k][0:64, :].rearrange("p (m n) -> p m n", m=2),
                        pip[0:64, 0:2, :]).then_inc(pil_done, 1)

            def normalise(b, k, c):
                oz = oz_bank[(k + c) % 2]
                dve.wait_ge(oz_ready, XC * b + c + 1)
                dve.wait_ge(seed_done, XC * b + c + 1)
                r, turn = XC * b + c, (k + c) % 2
                nc.vector.tensor_tensor(zr[:], oz[:, S:2 * S], rz[:, turn, :], ALU.mult).then_inc(zr_done, 1)
                dve.wait_ge(zr_done, r + 1)
                nc.vector.scalar_tensor_tensor(rz[:, turn, :], zr[:], -2.0, rz[:, turn, :],
                                               ALU.add, ALU.mult).then_inc(rz_done, 1)
                dve.wait_ge(rz_done, r + 1)
                if c == 0 and not (isinstance(b, int) and b == 0):
                    dve.wait_ge(on_done, XC * b)
                nc.vector.scalar_tensor_tensor(ot[:, c, :], oz[:, 0:S], -1.0, rz[:, turn, :],
                                               ALU.mult, ALU.mult).then_inc(ot_done, 1)

            def add_image(b, c):
                dve.wait_ge(ot_done, XC * b + c + 1)
                dve.wait_ge(oi_done, 2 * b + 1 + c // 2)
                nc.vector.tensor_tensor(on[:, c, :], ot[:, c, :], oi[:, c, :], ALU.add).then_inc(on_done, 1)

            def low_out(b, c):
                dve.wait_ge(onh_done, XC * b + c + 1)
                sub(on_l[:, c, :], on[:, c, :], on_h[:, c, :]).then_inc(onl_done, 1)

            def last_chunk_out(b):
                dve.wait_ge(onh_done, XC * (b + 1))
                if not (isinstance(b, int) and b == 0):
                    dve.wait_ge(out_ready, QT * b)
                nc.vector.scalar_tensor_tensor(on_l[:, 2, :], on_h[:, 2, :], con[:, NEG_SECOND:NEG_SECOND + 1],
                                               on[:, 2, :], ALU.mult, ALU.add).then_inc(onl_done, 1)

            def add_residual(b, t):
                dve.wait_ge(out_ready, QT * b + t + 1)
                if t == 0:
                    dve.wait_ge(xb_done, b + 1)
                    if not (isinstance(b, int) and b == 0):
                        dve.wait_ge(y_stored, 16 * b)
                nc.vector.tensor_tensor(y[:, t, :], spare[t][:, 0:D], xb[:, t, :], ALU.add).then_inc(y_done, 1)

            def step(b, k):
                c = b + 1
                reads = [n for n in range(2 * GROUPS) if exists(c)]

                def some_a(n):
                    for _ in range(n):
                        if reads:
                            read_a(c, reads.pop(0))

                some_a(2)
                if not exists(c):
                    last_chunk_out(b - 1)
                low_ip(b, k, 0)
                some_a(1)
                low_ip(b, k, 1)
                some_a(1)
                if exists(b + 2):
                    low_q(b + 2, 0)
                    low_q(b + 2, 1)
                some_a(1)
                if exists(b - 1) and exists(c):
                    last_chunk_out(b - 1)
                some_a(1)
                if exists(b + 3):
                    split_x(b + 3)
                some_a(4)
                if exists(c):
                    image_max(c)
                    low_shift(c)
                if exists(b - 1):
                    add_residual(b - 1, 0)
                    add_residual(b - 1, 1)
                normalise(b, k, 0)
                if exists(c):
                    image_sum(c)
                    normalise(b, k, 1)
                    normalise(b, k, 2)
                else:
                    add_image(b, 0)
                    normalise(b, k, 1)
                    low_out(b, 0)
                    add_image(b, 1)
                    normalise(b, k, 2)
                    low_out(b, 1)
                    add_image(b, 2)

            low_q(0, 0)
            low_q(0, 1)
            split_x(1)
            low_q(1, 0)
            low_q(1, 1)
            split_x(2)
            for n in range(2 * GROUPS):
                read_a(0, n)
            image_max(0)
            low_shift(0)
            image_sum(0)
            every_step(dve, step)
            last_chunk_out(B - 1)
            add_residual(B - 1, 0)
            add_residual(B - 1, 1)

        @block.gpsimd
        def _(pool):
            sub = lambda o, a, b: nc.gpsimd.tensor_tensor(o, a, b, ALU.subtract)
            for tile in (v[0], v[1], ipp, ks[0]):
                nc.gpsimd.memset(tile[:].bitcast(F32) if tile is ks[0] else tile[:], 0.0).then_inc(zeroed, 1)
            pool.wait_ge(con_in, 16)

            def ones(k):
                pool.wait_ge(zeroed, k + 4)
                for ab in range(2):
                    nc.gpsimd.tensor_copy(
                        ks[k][STACK:STACK + SHIFT, :, ab, :],
                        con[STACK:STACK + SHIFT, SHIFT_ROWS + ab:SHIFT_ROWS + ab + 1].unsqueeze(2)
                        .to_broadcast([SHIFT, PAIRS, KEYS])).then_inc(ones_set, 1)
                    pool.wait_ge(ones_set, 2 * k + ab + 1)

            def split_x(c):
                pool.wait_ge(xh_done, c + 1)
                sub(x_l[:, 0:2, :], x_raw[:, 0:2, :], x_h[:, 0:2, :]).then_inc(xl_done, 1)

            def image_values(c):
                pool.wait_ge(vr_in, 32)
                if not (isinstance(c, int) and c == 0):
                    pool.wait_ge(vip_done, c)
                nc.gpsimd.tensor_tensor(vm[:], vr[:, c], con[:, BLOCK:BLOCK + DP], ALU.mult).then_inc(vm_done, 1)
                if not (isinstance(c, int) and c == 0):
                    pool.wait_ge(oip_ready, 2 * c)
                pool.wait_ge(vm_done, c + 1)
                nc.gpsimd.tensor_tensor(vip_h[:], vm[:], con[:, BLOCK:BLOCK + DP], ALU.mult).then_inc(viph_done, 1)
                pool.wait_ge(viph_done, c + 1)
                sub(vip_l[:], vm[:], vip_h[:]).then_inc(vip_done, 1)

            def image_shift(c):
                pool.wait_ge(ipm_done, c + 1)
                if not (isinstance(c, int) and c == 0):
                    pool.wait_ge(ipe_done, c)
                nc.gpsimd.tensor_tensor(ipd[:], ips[:], ipm[:].unsqueeze(3).to_broadcast([P, QT, H, IP]),
                                        ALU.subtract).then_inc(ipd_done, 1)

            def image_norm(c):
                pool.wait_ge(ipr_done, c + 1)
                if not (isinstance(c, int) and c == 0):
                    pool.wait_ge(ipt_ready, 2 * c)
                nc.gpsimd.tensor_tensor(ipp[:, :, 0:H, :], ipe[:], ipr[:].unsqueeze(3).to_broadcast([P, QT, H, IP]),
                                        ALU.mult).then_inc(ipp_done, 1)

            def residual(b):
                pool.wait_ge(xres_in, 16 * (b + 1))
                if not (isinstance(b, int) and b == 0):
                    pool.wait_ge(y_done, QT * b)
                else:
                    pool.wait_ge(bias_in, 16)
                nc.gpsimd.tensor_tensor(xb[:], x_res[:], bias[:].unsqueeze(1).to_broadcast([P, QT, D]),
                                        ALU.add).then_inc(xb_done, 1)

            def output(b, c):
                pool.wait_ge(ot_done, XC * b + c + 1)
                pool.wait_ge(oi_done, 2 * b + 1 + c // 2)
                if c == 0 and not (isinstance(b, int) and b == 0):
                    pool.wait_ge(onl_done, XC * b)
                nc.gpsimd.tensor_tensor(on[:, c, :], ot[:, c, :], oi[:, c, :], ALU.add).then_inc(on_done, 1)
                if c < 2:
                    pool.wait_ge(onh_done, XC * b + c + 1)
                    sub(on_l[:, c, :], on[:, c, :], on_h[:, c, :]).then_inc(onl_done, 1)

            def step(b, k):
                if exists(b + 3):
                    split_x(b + 3)
                if exists(b + 1):
                    image_values(b + 1)
                    image_shift(b + 1)
                    output(b, 0)
                    image_norm(b + 1)
                    output(b, 1)
                    output(b, 2)
                residual(b)

            split_x(0)
            pool.wait_ge(xl_done, 2)
            ones(0)
            split_x(1)
            pool.wait_ge(vipn_ready, 1)
            nc.gpsimd.memset(ks[1][:].bitcast(F32), 0.0).then_inc(zeroed, 1)
            split_x(2)
            pool.wait_ge(xl_done, 6)
            ones(1)
            image_shift(0)
            image_norm(0)
            image_values(0)
            every_step(pool, step)


def kernel(x, ctx_2048, fside_Bx4x4_0, L0_xattn_w_q, L0_xattn_w_k, L0_xattn_w_v, L0_xattn_w_k_ip,
           L0_xattn_w_v_ip, L0_xattn_w_out, L0_xattn_b_out):
    import numpy as np
    import concourse.bacc as bacc
    from concourse.bass_utils import run_bass_kernel_spmd

    x, ctx_all, box = (np.ascontiguousarray(a) for a in (x, ctx_2048, fside_Bx4x4_0))
    wq, wk, wv, wk_ip, wv_ip, w_out, b_out = (np.ascontiguousarray(a) for a in (
        L0_xattn_w_q, L0_xattn_w_k, L0_xattn_w_v, L0_xattn_w_k_ip, L0_xattn_w_v_ip, L0_xattn_w_out, L0_xattn_b_out))

    def by_chunk(rows):
        return np.ascontiguousarray(rows.reshape(-1, P, rows.shape[1]).transpose(1, 0, 2))

    def padded(w):
        return np.pad(w, ((0, 0), (0, DP - D)))

    rows = np.r_[0:D, 2 * P:D]
    out_rows = np.r_[0:2 * P, np.concatenate([np.r_[h * DH:(h + 1) * DH, h * DH:(h + 1) * DH] for h in range(16, H)])]
    xT = x.transpose(0, 2, 1)[:, rows, :].reshape(B, XC, P, S).transpose(0, 2, 1, 3)
    arrays = {
        "xT": xT,
        "x": x,
        "ctxT": by_chunk(ctx_all[:, :TEXT].reshape(B * TEXT, C).T),
        "ctx_ipT": by_chunk(np.tile(ctx_all[:, TEXT:].transpose(2, 1, 0).reshape(C, IP * B), (1, 2))),
        "bbox": box.reshape(B * BOX * 4),
        "wq": by_chunk(padded(wq)[rows]),
        "wk": by_chunk(padded(wk)),
        "wv": by_chunk(wv),
        "wk_ip": by_chunk(padded(wk_ip)),
        "wv_ip": by_chunk(wv_ip[:, out_rows]),
        "w_out": by_chunk(w_out[out_rows]),
        "b_out": b_out,
        "consts": constants(),
    }
    nc = bacc.Bacc("TRN2", target_bir_lowering=False, num_devices=1)
    args = []
    for name, a in arrays.items():
        arrays[name] = a = np.ascontiguousarray(a)
        args.append(nc.dram_tensor(name, a.shape, mybir.dt.from_np(a.dtype), kind="ExternalInput").ap())
    args.append(nc.dram_tensor("out", (B, S, D), F32, kind="ExternalOutput").ap())
    build(nc, *args)
    r = run_bass_kernel_spmd(nc, [arrays], core_ids=[0])
    return r.results[0]["out"]
```

```python
from contextlib import ExitStack

import concourse.bass as bass
from concourse import mybir

F32 = mybir.dt.float32
F32R = mybir.dt.float32r
ALU = mybir.AluOpType
ACT = mybir.ActivationFunctionType
X = mybir.AxisListType.X

P = 128
B, S, D, C = 8, 256, 320, 512
H, DH = 20, 16
TEXT, IP = 112, 8
KEYS = TEXT + IP
BOX = IP // 2
GRID = 16
PAIRS = H // 2
QT = S // P
CC = C // P
XC = 3
DP = XC * P
GROUP = 4
GROUPS = H // GROUP
HPC = P // DH
SCALE = float(DH) ** -0.5
NEG = -10000.0 / SCALE
STACK = 3 * 32
SHIFT = 4

IDENT = 0
XG = IDENT + P
YG = XG + 1
NEG_SECOND = YG + QT
NEG_LOWER = NEG_SECOND + 1
SHIFT_ROWS = NEG_LOWER + 1
SUM_COLS = SHIFT_ROWS + 2
BLOCK = SUM_COLS + 3 * 32
CONSTS = BLOCK + DP


def constants():
    import numpy as np

    c = np.zeros((P, CONSTS), np.float32)
    p = np.arange(P)
    c[:, IDENT:IDENT + P] = np.eye(P)
    lin = np.linspace(0.0, 1.0, GRID, dtype=np.float32)
    c[:, XG] = lin[p % GRID]
    for t in range(QT):
        c[:, YG + t] = lin[(t * P + p) // GRID]
    c[:, NEG_SECOND] = -1.0 * (p % 32 >= DH)
    c[:, NEG_LOWER] = -1.0 * (p >= 64)
    for r in range(SHIFT):
        c[STACK + r, SHIFT_ROWS + r % 2] = 1.0
    c[:, SUM_COLS:SUM_COLS + DH] = 1.0
    c[:, SUM_COLS + 32 + DH:SUM_COLS + 64] = 1.0
    c[:, SUM_COLS + 64:SUM_COLS + 96] = 1.0
    head = p % (HPC * IP) // IP
    for j in range(XC):
        d = np.arange(P)
        own = d // DH if j < 2 else d // 32
        c[:, BLOCK + j * P:BLOCK + (j + 1) * P] = head[:, None] == own[None, :]
    return c


def build(nc, xT, x, ctxT, ctx_ipT, bbox, wq, wk, wv, wk_ip, wv_ip, w_out, b_out, consts, out):
    ctx = ExitStack()
    with ctx:
        def sb(name, shape, dt=F32):
            return ctx.enter_context(nc.sbuf_tensor(name, shape, dt))

        def sem(name):
            return ctx.enter_context(nc.semaphore(name))

        k_dram = nc.dram_tensor("k_dram", (2, PAIRS, 2, DH, B, KEYS), F32, kind="Internal").ap()
        vip_dram = nc.dram_tensor("vip_dram", (IP, B, DP), F32, kind="Internal").ap()
        q_dram = nc.dram_tensor("q_dram", (2, 2, DP // 32, 32, S), F32, kind="Internal").ap()

        shift_dram = nc.dram_tensor("shift_dram", (2, 2, PAIRS, S), F32, kind="Internal").ap()

        con = sb("con", [P, CONSTS])
        ident = con[:, IDENT:IDENT + P]
        raw = sb("raw", [P, PAIRS * 2 * S + B * D])
        w_raw = raw[:, 0:2 * CC * DP].rearrange("p (s j n) -> p s j n", s=2, j=CC)
        ctx_raw = raw[:, 2 * CC * DP:2 * CC * DP + CC * B * TEXT].rearrange("p (j n) -> p j n", j=CC)
        probs = raw[0:TEXT, 0:PAIRS * 2 * S].rearrange("p (a n) -> p a n", a=PAIRS)
        v_all = raw[0:TEXT, PAIRS * 2 * S:].rearrange("p (b h d) -> p b h d", b=B, h=H)
        ctx_hl = sb("ctx_hl", [P, 2, CC * B * TEXT], F32R)
        ctx_h, ctx_l = (ctx_hl[:, n].rearrange("p (j n) -> p j n", j=CC) for n in range(2))
        vr = ctx_hl[:, 0, 0:B * DP].bitcast(F32).rearrange("p (b n) -> p b n", b=B)
        cip_raw = sb("cip_raw", [P, CC, P])
        cip_h, cip_l = (sb(n, [P, CC, P], F32R) for n in ("cip_h", "cip_l"))
        key_w = sb("key_w", [P, 4, CC * DP], F32R)
        wk_h, wk_l, wkip_h, wkip_l = (key_w[:, n].rearrange("p (j n) -> p j n", j=CC) for n in range(4))
        key_w_flat = key_w[:].rearrange("p s n -> p (s n)")
        wq_h, wq_l = (sb(n, [P, XC, DP], F32R) for n in ("wq_h", "wq_l"))
        wv_h, wv_l = (sb(n, [P, CC, D], F32R) for n in ("wv_h", "wv_l"))
        wo_h, wo_l = (sb(n, [P, XC, D], F32R) for n in ("wo_h", "wo_l"))
        late = sb("late", [P, 3 * XC * S + 2 * QT * D + 2 * S])
        ot, oi, on = (late[:, n * XC * S:(n + 1) * XC * S].rearrange("p (c n) -> p c n", c=XC) for n in range(3))
        at_x = 3 * XC * S
        x_res, y = (late[:, at_x + n * QT * D:at_x + (n + 1) * QT * D].rearrange("p (t n) -> p t n", t=QT)
                    for n in range(2))
        rz = late[:, at_x + 2 * QT * D:].rearrange("p (k n) -> p k n", k=2)
        kc_more = sb("kc_more", [P, 2, B * KEYS])
        kc = [late[:, n * B * KEYS:(n + 1) * B * KEYS] for n in range(4)] + [kc_more[:, n] for n in range(2)]
        kc = [t.bitcast(F32R).rearrange("p (b n) -> p b n", b=B) for t in kc]
        kc_h, kc_l = kc[0:XC], kc[XC:]
        box = sb("box", [P, B, BOX, 4])
        inside = sb("inside", [P, QT, B, BOX])
        some = sb("some", [P, QT, B])
        mask = sb("mask", [P, QT, B, IP])
        bias = sb("bias", [P, D])

        x_raw = sb("x_raw", [P, XC, S])
        x_h, x_l = (sb(n, [P, XC, S], F32R) for n in ("x_h", "x_l"))
        q_h, q_l = (sb(n, [P, XC, S], F32R) for n in ("q_h", "q_l"))
        qs = [sb("qs0", [P, PAIRS, S], F32R),
              key_w_flat[:, 2 * CC * DP:2 * CC * DP + PAIRS * S].rearrange("p (a n) -> p a n", a=PAIRS)]
        ks = [sb("ks0", [P, PAIRS, 2, KEYS], F32R),
              key_w_flat[:, 0:PAIRS * 2 * KEYS].rearrange("p (a s n) -> p a s n", a=PAIRS, s=2)]
        v = [sb(f"v{k}", [TEXT, H, 32]) for k in range(2)]
        negmax = sb("negmax", [P, QT, 2, PAIRS])
        shift = sb("shift", [H, 2, S], F32R)
        ips = sb("ips", [P, QT, H, IP])
        ipd = sb("ipd", [P, QT, H, IP])
        ipe = sb("ipe", [P, QT, H, IP])
        ipm = sb("ipm", [P, QT, H])
        ipz = sb("ipz", [P, QT, H])
        ipr = sb("ipr", [P, QT, H])
        ipp = sb("ipp", [P, QT, XC * HPC, IP])
        pip = sb("pip", [P, XC, S], F32R)
        vipn = sb("vipn", [B * IP, DP])
        vm = sb("vm", [P, DP])
        vip_h, vip_l = (sb(n, [P, DP], F32R) for n in ("vip_h", "vip_l"))
        on_h, on_l = (ctx_hl[:, 1, n * XC * S:(n + 1) * XC * S].rearrange("p (c n) -> p c n", c=XC) for n in range(2))
        log_z = sb("log_z", [P, 2, S])
        zr = sb("zr", [P, S])
        xb = sb("xb", [P, QT, D])

        bank = [ctx.enter_context(nc.psum_tensor(f"bank{i}", [P, 512], F32)) for i in range(8)]
        a_bank = bank[0:2]
        b_bank = bank[2:4]
        oz_bank = bank[4:6]
        spare = bank[6:8]
        v_bank = bank[2:6]

        wk_ctx_in = [sem(f"wk_ctx_in{j}") for j in range(CC)]
        kip_in, vip_w_in, wq_in, wv_in, wo_in = (sem(n) for n in ("kip_in", "vip_w_in", "wq_in", "wv_in", "wo_in"))
        con_in, box_in, bias_in = (sem(n) for n in ("con_in", "box_in", "bias_in"))
        x_in, xres_in, ks_in, vr_first_in, vr_in = (
            sem(n) for n in ("x_in", "xres_in", "ks_in", "vr_first_in", "vr_in"))
        high, low = sem("high"), sem("low")
        zeroed, ones_set, mask_ready, mask_step = (sem(n) for n in ("zeroed", "ones_set", "mask_ready", "mask_step"))
        k_ready, kh_done, kl_done, k_stored = (sem(n) for n in ("k_ready", "kh_done", "kl_done", "k_stored"))
        vipn_ready, vipn_done, vipn_stored = (sem(n) for n in ("vipn_ready", "vipn_done", "vipn_stored"))
        xh_done, xl_done = sem("xh_done"), sem("xl_done")
        q_ready, qh_done, ql_done, q_stored, qs_in = (
            sem(n) for n in ("q_ready", "qh_done", "ql_done", "q_stored", "qs_in"))
        va_ready, va_done, v_done = sem("va_ready"), sem("va_done"), sem("v_done")
        a_ready, a_max, a_used = sem("a_ready"), sem("a_max"), sem("a_used")
        shift_ready, sh_done, sl_done, shift_in = (sem(n) for n in ("shift_ready", "sh_done", "sl_done", "shift_in"))
        shift_stored = sem("shift_stored")
        ipm_done, ipd_done, ipe_done, ipz_done, ipr_done, ipp_done = (
            sem(n) for n in ("ipm_done", "ipd_done", "ipe_done", "ipz_done", "ipr_done", "ipp_done"))
        ipt_ready, pih_done, pil_done = sem("ipt_ready"), sem("pih_done"), sem("pil_done")
        vm_done, viph_done, vip_done = sem("vm_done"), sem("viph_done"), sem("vip_done")
        oip_ready, oi_done = sem("oip_ready"), sem("oi_done")
        b_ready, p_done, z_ready, oz_ready = (sem(n) for n in ("b_ready", "p_done", "z_ready", "oz_ready"))
        log_done, seed_done, zr_done, rz_done = (sem(n) for n in ("log_done", "seed_done", "zr_done", "rz_done"))
        ot_done, on_done, onh_done, onl_done = (sem(n) for n in ("ot_done", "on_done", "onh_done", "onl_done"))
        out_ready, xb_done, y_done, y_stored = (sem(n) for n in ("out_ready", "xb_done", "y_done", "y_stored"))

        splits = []
        for j in range(CC):
            splits.append((wk_ctx_in[j], 32, wk_h[:, j, :], wk_l[:, j, :], w_raw[:, 0, j, :]))
            splits.append((wk_ctx_in[j], 32, ctx_h[:, j, :], ctx_l[:, j, :], ctx_raw[:, j, :]))
        splits.append((kip_in, 32, cip_h[:], cip_l[:], cip_raw[:]))
        splits.append((kip_in, 32, wkip_h[:], wkip_l[:], w_raw[:, 1]))
        K_SPLIT = len(splits)
        splits.append((wq_in, 16, wq_h[:], wq_l[:], w_raw[:, 0, 0:XC, :]))
        Q_SPLIT = len(splits)
        splits.append((wv_in, 16, wv_h[:], wv_l[:], w_raw[:, 1, :, 0:D]))
        V_SPLIT = len(splits)
        splits.append((vip_w_in, 16, wkip_h[:], wkip_l[:], ctx_raw[:, :, 0:DP]))
        VIP_SPLIT = len(splits)
        splits.append((wo_in, 16, wo_h[:], wo_l[:], ctx_raw[:, 0:XC, DP:DP + D]))
        wo_raw = ctx_raw[:, 0:XC, DP:DP + D]
        wvip_h, wvip_l, wvip_raw = wkip_h, wkip_l, ctx_raw[:, :, 0:DP]

        def chunk_heads(c):
            if c < 2:
                return [(j, 4 * c + j, ab, ab) for ab in range(2) for j in range(4)]
            return [(j, 8 + j // 2, j % 2, 2) for j in range(4)]

        def exists(b):
            return not isinstance(b, int) or 0 <= b < B

        def b_banks(b):
            return b_bank if exists(b + 1) else b_bank + a_bank

        def sums_apart(b, c):
            return not exists(b + 1) and c > 0

        def sums(b, k, c):
            return a_bank[c - 1][:, 0:S] if sums_apart(b, c) else oz_bank[(k + c) % 2][:, S:2 * S]

        def ip_bank(b, k, part):
            return oz_bank[(k + part) % 2] if exists(b + 2) else spare[part]

        def every_step(engine, step):
            step(0, 0)
            with engine.Fori(0, (B - 4) // 2) as i:
                step(2 * i + 1, 1)
                step(2 * i + 2, 0)
            for b in range(B - 3, B):
                step(b, b % 2)

        block = ctx.enter_context(nc.Block())

        @block.sync
        def _(sp):
            for j in range(CC):
                sp.dma_start(w_raw[:, 0, j, :], wk[:, j, :]).then_inc(wk_ctx_in[j], 16)
                sp.dma_start(ctx_raw[:, j, :], ctxT[:, j, :]).then_inc(wk_ctx_in[j], 16)
            sp.dma_start(cip_raw[:], ctx_ipT).then_inc(kip_in, 16)
            sp.dma_start(w_raw[:, 1], wk_ip).then_inc(kip_in, 16)
            sp.dma_start(con[:], consts).then_inc(con_in, 16)
            sp.dma_start(x_raw[:], xT[0]).then_inc(x_in, 16)
            sp.dma_start(box[:].rearrange("p b m c -> p (b m c)"), bbox.partition_broadcast(P)).then_inc(box_in, 16)
            sp.dma_start(bias[:], b_out.partition_broadcast(P)).then_inc(bias_in, 16)
            sp.wait_ge(high, 2 * CC)
            sp.wait_ge(low, 2 * CC)
            sp.dma_start(w_raw[:, 0, 0:XC, :], wq).then_inc(wq_in, 16)
            sp.dma_start(wo_raw, w_out).then_inc(wo_in, 16)
            sp.wait_ge(high, K_SPLIT)
            sp.wait_ge(low, K_SPLIT)
            sp.dma_start(w_raw[:, 1, :, 0:D], wv).then_inc(wv_in, 16)
            sp.dma_start(ctx_raw[:, :, 0:DP], wv_ip).then_inc(vip_w_in, 16)

            def keys(c, k, blk):
                for ab in range(2):
                    r = 32 * blk + DH * ab
                    sp.dma_start(ks[k][r:r + DH, :, ab, :].bitcast(F32),
                                 k_dram[blk % 2, :, ab, :, c, :].rearrange("p d n -> d p n")).then_inc(ks_in, 16)

            def store_queries(c, k):
                if not (isinstance(c, int) and c < 2):
                    sp.wait_ge(qs_in, 16 * 3 * (c - 1))
                for part, (done, tile) in enumerate(((qh_done, q_h), (ql_done, q_l))):
                    sp.wait_ge(done, 2 * (c + 1))
                    sp.dma_start(q_dram[k, part].rearrange("(m j) r n -> (j r) m n", m=XC),
                                 tile[:].bitcast(F32)).then_inc(q_stored, 16)

            def queries(c, k):
                sp.wait_ge(q_stored, 16 * 2 * (c + 1))
                for blk, part in enumerate((0, 0, 1)):
                    sp.dma_start(qs[k][32 * blk:32 * blk + 32, :, :].bitcast(F32),
                                 q_dram[k, part, 0:PAIRS].rearrange("a r n -> r a n")).then_inc(qs_in, 16)

            def store_shifts(c):
                if not (isinstance(c, int) and c == 0):
                    sp.wait_ge(shift_in, 16 * c)
                sp.wait_ge(sh_done, c + 1)
                sp.wait_ge(sl_done, c + 1)
                sp.dma_start(shift_dram.rearrange("s a p n -> (a p) s n"),
                             shift[:].bitcast(F32)).then_inc(shift_stored, 16)

            def shifts(c, k):
                sp.wait_ge(shift_stored, 16 * (c + 1))
                sp.dma_start(qs[k][STACK:STACK + SHIFT, :, :].bitcast(F32),
                             shift_dram.rearrange("s a p n -> (s a) p n")).then_inc(shift_in, 16)

            def store(b):
                sp.wait_ge(y_done, QT * (b + 1))
                sp.dma_start(out[b].rearrange("(t p) d -> p t d", p=P), y[:]).then_inc(y_stored, 16)

            def residual(b):
                if not (isinstance(b, int) and b == 0):
                    sp.wait_ge(xb_done, b)
                sp.dma_start(x_res[:], x[b].rearrange("(t p) d -> p t d", p=P)).then_inc(xres_in, 16)

            def load_x(c):
                sp.wait_ge(xl_done, 2 * c)
                sp.wait_ge(xh_done, c)
                sp.dma_start(x_raw[:], xT[c]).then_inc(x_in, 16)

            def step(b, k):
                if exists(b - 1) and exists(b + 3):
                    load_x(b + 3)
                residual(b)
                if exists(b + 2):
                    store_queries(b + 2, k)
                if exists(b + 2):
                    sp.wait_ge(b_ready, PAIRS * (b + 1))
                    keys(b + 2, k, 0)
                    keys(b + 2, k, 1)
                if exists(b + 1):
                    store_shifts(b + 1)
                if exists(b + 2):
                    queries(b + 2, k)
                shifts_first = not (exists(b - 1) and exists(b + 3))
                if exists(b + 1) and shifts_first:
                    shifts(b + 1, 1 - k)
                if exists(b + 2):
                    keys(b + 2, k, 2)
                if exists(b + 1) and not shifts_first:
                    shifts(b + 1, 1 - k)
                if exists(b - 1):
                    store(b - 1)

            load_x(1)

            def store_keys(m, batches):
                n = min(P, D - m * P)
                for part, tile in enumerate((kc_h[m], kc_l[m])):
                    sp.dma_start(k_dram[part].rearrange("p a d b n -> (p a d) b n")[m * P:m * P + n, batches],
                                 tile[0:n, batches].bitcast(F32)).then_inc(k_stored, 16)

            for m in range(XC):
                sp.wait_ge(kh_done, 2 * m + 3)
                sp.wait_ge(kl_done, 2 * m + 3)
                store_keys(m, slice(0, 2))
            store_queries(0, 0)
            sp.wait_ge(zeroed, 4)
            sp.wait_ge(k_stored, 16 * 2 * XC)
            for blk in range(3):
                keys(0, 0, blk)
            queries(0, 0)
            store_keys(0, slice(2, B))
            sp.wait_ge(zeroed, 5)
            sp.wait_ge(ks_in, 16 * 6)
            for blk in range(3):
                keys(1, 1, blk)
            store_queries(1, 1)
            load_x(2)
            sp.wait_ge(qs_in, 16 * 3)
            sp.wait_ge(vipn_done, 1)
            queries(1, 1)
            sp.dma_start(vip_dram.rearrange("k b n -> (k b) n"), vipn[:]).then_inc(vipn_stored, 16)
            sp.wait_ge(va_ready, B)
            sp.wait_ge(vipn_stored, 16)

            def load_vr(batches, loaded):
                for n in range(2):
                    sp.dma_start(vr[64 * n:64 * n + 64, batches],
                                 vip_dram[:, batches].unsqueeze(0).to_broadcast([HPC, IP, batches.stop - batches.start, DP])
                                 ).then_inc(loaded, 16)

            load_vr(slice(0, 1), vr_first_in)
            store_shifts(0)
            store_keys(1, slice(2, B))
            shifts(0, 0)
            load_x(3)
            store_keys(2, slice(2, B))
            load_vr(slice(1, B), vr_in)
            sp.wait_ge(k_stored, 16 * 4 * XC)
            every_step(sp, step)
            store(B - 1)
            sp.wait_ge(y_stored, 16 * B)

        @block.tensor
        def _(pe):
            def three(out_ap, products, start=True, stop=True):
                for n, (lhsT, rhs) in enumerate(products):
                    mm = pe.matmul(out_ap, lhsT, rhs, start=start and n == 0, stop=stop and n == len(products) - 1)
                return mm

            def image_keys():
                pe.wait_ge(high, K_SPLIT)
                pe.wait_ge(low, K_SPLIT)
                for m in range(XC):
                    mm = three(spare[0][:, 64 * m:64 * m + 64],
                               [(w[:, j, m * P:(m + 1) * P], t[:, j, 0:B * IP]) for j in range(CC)
                                for w, t in ((wkip_h, cip_h), (wkip_h, cip_l), (wkip_l, cip_h))])
                mm.then_inc(k_ready, 1)

            for j in range(CC):
                if j == CC - 1:
                    image_keys()
                pe.wait_ge(high, 2 * j + 2)
                pe.wait_ge(low, 2 * j + 2)
                for m in range(XC):
                    w_hi, w_lo = (w[:, j, m * P:(m + 1) * P] for w in (wk_h, wk_l))
                    for half in range(2):
                        n = slice(half * 448, half * 448 + 448)
                        mm = three(bank[2 * m + half][:, 0:448],
                                   [(w_hi, ctx_h[:, j, n]), (w_hi, ctx_l[:, j, n]), (w_lo, ctx_h[:, j, n])],
                                   start=j == 0, stop=j == CC - 1)
                        if j == CC - 1:
                            mm.then_inc(k_ready, 1)

            def image_values():
                pe.wait_ge(high, VIP_SPLIT)
                pe.wait_ge(low, VIP_SPLIT)
                three(spare[1][:, 0:DP],
                      [(t[:, j, :], w[:, j, :]) for j in range(CC)
                       for t, w in ((cip_h, wvip_h), (cip_h, wvip_l), (cip_l, wvip_h))]).then_inc(vipn_ready, 1)

            def project_q(c):
                pe.wait_ge(xh_done, c + 1)
                pe.wait_ge(xl_done, 2 * (c + 1))
                for m in range(XC):
                    cols = slice(m * P, (m + 1) * P)
                    prods = [(w[:, j, cols], t[:, j, :]) for j in range(2)
                             for w, t in ((wq_h, x_h), (wq_h, x_l), (wq_l, x_h))]
                    prods += [(wq_h[:, 2, cols], x_l[:, 2, :]), (wq_l[:, 2, cols], x_l[:, 2, :])]
                    mm = three(spare[m // 2][:, S * (m % 2):S * (m % 2) + S], prods)
                    if m:
                        mm.then_inc(q_ready, 1)

            def project_v(b):
                if b >= 4:
                    pe.wait_ge(va_done, b - 3)
                n = slice(b * TEXT, (b + 1) * TEXT)
                three(v_bank[b % 4][0:TEXT, 0:D],
                      [(t[:, j, n], w[:, j, :]) for j in range(CC)
                       for t, w in ((ctx_h, wv_h), (ctx_h, wv_l), (ctx_l, wv_h))]).then_inc(va_ready, 1)

            def score_a(c, k, n):
                if n == 0:
                    pe.wait_ge(qs_in, 16 * 3 * (c + 1))
                    pe.wait_ge(ks_in, 16 * 6 * (c + 1))
                t, g = n // GROUPS, n % GROUPS
                if n >= 2 or not (isinstance(c, int) and c == 0):
                    pe.wait_ge(a_used, 2 * GROUPS * c + n - 1)
                for p in range(2):
                    mm = pe.matmul(a_bank[n % 2][:, 2 * KEYS * p:2 * KEYS * (p + 1)],
                                   qs[k][0:STACK, 2 * g + p, t * P:(t + 1) * P],
                                   ks[k][0:STACK, 2 * g + p, :, :].rearrange("p a n -> p (a n)"),
                                   start=True, stop=True)
                mm.then_inc(a_ready, 1)

            def transpose_max(c):
                pe.wait_ge(a_max, 2 * GROUPS * (c + 1))
                for t in range(QT):
                    mm = pe.transpose(spare[1][0:H, t * P:(t + 1) * P], negmax[:, t].rearrange("p a n -> p (a n)"), ident)
                mm.then_inc(shift_ready, 1)

            def score_b(b, k, p):
                if p == 0:
                    pe.wait_ge(shift_in, 16 * (b + 1))
                banks = b_banks(b)
                if p >= len(banks):
                    pe.wait_ge(p_done, PAIRS * b + p + 1 - len(banks))
                elif p < 2 and not (isinstance(b, int) and b == 0):
                    pe.wait_ge(p_done, PAIRS * b + p - 1)
                for ab in range(2):
                    mm = pe.matmul(banks[p % len(banks)][0:TEXT, S * ab:S * ab + S],
                                   ks[k][0:STACK + SHIFT, p, ab, 0:TEXT],
                                   qs[k][0:STACK + SHIFT, p, :], start=True, stop=True)
                mm.then_inc(b_ready, 1)

            def transpose_ip(b, k, part):
                if part == 0:
                    pe.wait_ge(con_in, 16)
                    pe.wait_ge(ipp_done, b + 1)
                for c in (2,) if part == 0 else (0, 1):
                    for t in range(QT):
                        at = S * (c % 2) + t * P
                        mm = pe.transpose(ip_bank(b, k, part)[0:HPC * IP, at:at + P],
                                          ipp[:, t, HPC * c:HPC * (c + 1), :].rearrange("p h n -> p (h n)"), ident)
                mm.then_inc(ipt_ready, 1)

            def image_out(b, part):
                if part == 0:
                    pe.wait_ge(pih_done, 2 * (b + 1))
                    pe.wait_ge(pil_done, 2 * (b + 1))
                    pe.wait_ge(vip_done, b + 1)
                for c in (0, 1) if part == 0 else (2,):
                    cols = slice(c * P, (c + 1) * P)
                    mm = three(spare[1 - part][:, S * (c % 2):S * (c % 2) + S],
                               [(w[:, cols], pip[:, c, :]) for w in (vip_h, vip_l)])
                mm.then_inc(oip_ready, 1)

            def text_out(b, k, c):
                pe.wait_ge(p_done, PAIRS * b + (4, 8, 10)[c])
                if c == 0:
                    pe.wait_ge(v_done, b + 1)
                if c < 2 and exists(b + 2):
                    pe.wait_ge(pil_done, 2 * b + c + 1)
                if c == 2 or not (isinstance(b, int) and b == 0):
                    pe.wait_ge(ot_done, XC * b + c - 1)
                heads = chunk_heads(c)
                for n, (j, p, ab, _) in enumerate(heads):
                    mm = pe.matmul(oz_bank[(k + c) % 2][32 * j:32 * j + 32, 0:S], v[k][:, 2 * p + ab, :],
                                   probs[:, p, S * ab:S * ab + S],
                                   start=n < 4, stop=n >= len(heads) - 4, skip_group_check=True)
                if sums_apart(b, c):
                    mm.then_inc(oz_ready, 1)

            def text_sums(b, k, c):
                apart = sums_apart(b, c)
                if apart:
                    pe.wait_ge(p_done, PAIRS * b + (4, 8, 10)[c])
                heads = chunk_heads(c)
                for n, (j, p, ab, cols) in enumerate(heads):
                    mm = pe.matmul(sums(b, k, c)[32 * j:32 * j + 32, :],
                                   con[0:TEXT, SUM_COLS + 32 * cols:SUM_COLS + 32 * cols + 32],
                                   probs[:, p, S * ab:S * ab + S],
                                   start=apart and n < 4, stop=n >= len(heads) - 4, skip_group_check=True)
                mm.then_inc(z_ready if apart else oz_ready, 1)

            def project_out(b, t, chunks=range(XC)):
                q = slice(t * P, (t + 1) * P)
                for j in chunks:
                    if t == 0:
                        pe.wait_ge(onh_done, XC * b + j + 1)
                        pe.wait_ge(onl_done, XC * b + j + 1)
                    prods = (((on_h, wo_h), (on_h, wo_l), (on_l, wo_h)) if j < XC - 1 else
                             ((on_l, wo_h), (on_l, wo_l)))
                    mm = three(spare[t][:, 0:D], [(o[:, j, q], w[:, j, :]) for o, w in prods],
                               start=j == 0, stop=j == XC - 1)
                if j == XC - 1:
                    mm.then_inc(out_ready, 1)

            def step(b, k):
                c = b + 1
                if exists(b - 1) and exists(b + 2):
                    pe.wait_ge(sl_done, c)
                    pe.wait_ge(oi_done, 2 * b)
                    pe.wait_ge(ot_done, XC * b - 2)
                    project_q(b + 2)
                a = [n for n in range(2 * GROUPS) if exists(c)]

                def more_a(n):
                    for _ in range(n):
                        score_a(c, 1 - k, a.pop(0))

                def both(p):
                    more_a(1)
                    score_b(b, k, p)

                if not exists(b - 1):
                    more_a(2)
                    pe.wait_ge(sl_done, c)
                    project_q(b + 2)
                    transpose_ip(b, k, 0)
                    transpose_ip(b, k, 1)
                    more_a(2)
                    for p in range(4):
                        score_b(b, k, p)
                else:
                    score_b(b, k, 0)
                    if exists(b + 2):
                        pe.wait_ge(ot_done, XC * b)
                    else:
                        pe.wait_ge(y_done, QT * (b - 1))
                        pe.wait_ge(sl_done, c)
                    if exists(b + 2):
                        more_a(1)
                        both(1)
                        transpose_ip(b, k, 0)
                        transpose_ip(b, k, 1)
                        both(2)
                        both(3)
                    elif exists(c):
                        score_b(b, k, 1)
                        more_a(2)
                        transpose_ip(b, k, 0)
                        transpose_ip(b, k, 1)
                        both(2)
                        both(3)
                    else:
                        for p in (1, 2, 3):
                            score_b(b, k, p)
                        transpose_ip(b, k, 0)
                        transpose_ip(b, k, 1)
                if not exists(c):
                    last_step(b, k)
                    return
                both(4)
                text_out(b, k, 0)
                both(5)
                text_sums(b, k, 0)
                both(6)
                if exists(b + 2):
                    pe.wait_ge(ql_done, 2 * (b + 3))
                image_out(b, 0)
                both(7)
                image_out(b, 1)
                both(8)
                both(9)
                pe.wait_ge(oi_done, 2 * b + 1)
                transpose_max(c)
                if exists(b - 1):
                    pe.wait_ge(oi_done, 2 * b + 2)
                    project_out(b - 1, 0)
                    pe.wait_ge(sl_done, c + 1)
                    project_out(b - 1, 1)
                for chunk in (1, 2):
                    text_out(b, k, chunk)
                    text_sums(b, k, chunk)

            def last_step(b, k):
                score_b(b, k, 4)
                score_b(b, k, 5)
                text_out(b, k, 0)
                score_b(b, k, 6)
                score_b(b, k, 7)
                text_sums(b, k, 0)
                score_b(b, k, 8)
                pe.wait_ge(pil_done, 2 * (b + 1))
                project_out(b - 1, 0)
                score_b(b, k, 9)
                project_out(b - 1, 1)
                text_sums(b, k, 1)
                pe.wait_ge(y_done, QT * b)
                image_out(b, 0)
                image_out(b, 1)
                text_out(b, k, 1)
                text_sums(b, k, 2)
                text_out(b, k, 2)

            pe.wait_ge(high, Q_SPLIT)
            pe.wait_ge(low, Q_SPLIT)
            pe.wait_ge(kl_done, 1)
            project_q(0)
            pe.wait_ge(high, V_SPLIT)
            pe.wait_ge(low, V_SPLIT)
            pe.wait_ge(kl_done, 7)
            for b in range(3):
                project_v(b)
            pe.wait_ge(ql_done, 2)
            image_values()
            project_v(3)
            pe.wait_ge(vipn_done, 1)
            project_q(1)
            for n in range(2 * GROUPS):
                score_a(0, 0, n)
                if n % 2 and n < 8:
                    project_v(4 + n // 2)
            pe.wait_ge(ql_done, 4)
            pe.wait_ge(va_done, B)
            pe.wait_ge(con_in, 16)
            transpose_max(0)
            pe.wait_ge(low, len(splits))
            pe.wait_ge(ones_set, 4)
            every_step(pe, step)
            pe.wait_ge(oi_done, 2 * B)
            for j in range(XC):
                for t in range(QT):
                    project_out(B - 1, t, [j])

        @block.scalar
        def _(act):
            copy = nc.scalar.copy
            nc.scalar.preload_act_table_set("natural_log_exp_and_others")

            def split(n):
                loaded, count, hi, _, raw = splits[n]
                act.wait_ge(loaded, count)
                copy(hi, raw).then_inc(high, 1)

            def split_x(c):
                act.wait_ge(x_in, 16 * (c + 1))
                copy(x_h[:], x_raw[:]).then_inc(xh_done, 1)

            for n in range(K_SPLIT):
                split(n)
            split_x(0)
            split(Q_SPLIT - 1)
            split(V_SPLIT - 1)
            act.wait_ge(k_ready, 1)
            for m in range(XC):
                mm = copy(kc_h[m][:, :, TEXT:KEYS],
                          spare[0][:, 64 * m:64 * m + 64].rearrange("p (n b) -> p b n", b=B))
            mm.then_inc(kh_done, 1)
            for m in range(XC):
                for half in range(2):
                    act.wait_ge(k_ready, 2 * m + half + 2)
                    copy(kc_h[m][:, 4 * half:4 * half + 4, 0:TEXT],
                         bank[2 * m + half][:, 0:448].rearrange("p (b n) -> p b n", b=4)).then_inc(kh_done, 1)
            split(VIP_SPLIT - 1)
            split(VIP_SPLIT)

            def high_q(c, part):
                act.wait_ge(q_ready, 2 * c + part + 1)
                if part == 0 and not (isinstance(c, int) and c == 0):
                    act.wait_ge(q_stored, 32 * c)
                if part == 0:
                    copy(q_h[:, 0:2, :], spare[0][:].rearrange("p (m n) -> p m n", m=2)).then_inc(qh_done, 1)
                else:
                    copy(q_h[:, 2, :], spare[1][:, 0:S]).then_inc(qh_done, 1)

            def values(c, k):
                if not (isinstance(c, int) and c < 2):
                    act.wait_ge(oz_ready, XC * (c - 1))
                src = v_all[:, c]
                copy(v[k][:, 0:16:2, 0:DH], src[:, 0:16:2, :])
                copy(v[k][:, 1:16:2, DH:32], src[:, 1:16:2, :])
                copy(v[k][:, 16:H, 0:DH], src[:, 16:H, :])
                copy(v[k][:, 16:H, DH:32], src[:, 16:H, :]).then_inc(v_done, 1)

            def high_shift(c):
                act.wait_ge(shift_ready, c + 1)
                if not (isinstance(c, int) and c == 0):
                    act.wait_ge(shift_stored, 16 * c)
                copy(shift[:, 0], spare[1][0:H, 0:S]).then_inc(sh_done, 1)

            def image_exp(c):
                act.wait_ge(ipd_done, c + 1)
                if not (isinstance(c, int) and c == 0):
                    act.wait_ge(ipp_done, c)
                nc.scalar.activation(ipe[:], ipd[:], ACT.Exp, scale=SCALE).then_inc(ipe_done, 1)

            def probabilities(b, p):
                act.wait_ge(b_ready, PAIRS * b + p + 1)
                if p in (0, 4, 8) and not (isinstance(b, int) and b == 0):
                    act.wait_ge(oz_ready, XC * (b - 1) + p // 4 + 1)
                nc.scalar.activation(probs[:, p, :], b_banks(b)[p % len(b_banks(b))][0:TEXT, :], ACT.Exp,
                                     scale=SCALE).then_inc(p_done, 1)

            def high_ip(b, k, part):
                act.wait_ge(ipt_ready, 2 * b + part + 1)
                if part == 0:
                    if not (isinstance(b, int) and b == 0):
                        act.wait_ge(oip_ready, 2 * b)
                    copy(pip[0:64, 2, :], ip_bank(b, k, 0)[0:64, 0:S]).then_inc(pih_done, 1)
                else:
                    copy(pip[0:64, 0:2, :],
                         ip_bank(b, k, 1)[0:64, :].rearrange("p (m n) -> p m n", m=2)).then_inc(pih_done, 1)

            def image_part(b, part):
                act.wait_ge(oip_ready, 2 * b + part + 1)
                if part == 0:
                    if not (isinstance(b, int) and b == 0):
                        act.wait_ge(on_done, XC * b)
                    copy(oi[:, 0:2, :], spare[1][:].rearrange("p (m n) -> p m n", m=2)).then_inc(oi_done, 1)
                else:
                    copy(oi[:, 2, :], spare[0][:, 0:S]).then_inc(oi_done, 1)

            def high_out(b, c):
                act.wait_ge(on_done, XC * b + c + 1)
                if c == 0 and not (isinstance(b, int) and b == 0):
                    act.wait_ge(out_ready, QT * b)
                copy(on_h[:, c, :], on[:, c, :]).then_inc(onh_done, 1)

            def seed(b, k, c):
                turn = (k + c) % 2
                if sums_apart(b, c):
                    act.wait_ge(z_ready, c)
                else:
                    act.wait_ge(oz_ready, XC * b + c + 1)
                if isinstance(b, int) and b == 0 and c == 0:
                    act.wait_ge(k_stored, 16 * 4 * XC)
                if c == 2 or not (isinstance(b, int) and b == 0):
                    act.wait_ge(ot_done, XC * b + c - 1)
                nc.scalar.activation(log_z[:, turn, :], sums(b, k, c), ACT.Ln).then_inc(log_done, 1)
                act.wait_ge(log_done, XC * b + c + 1)
                nc.scalar.activation(rz[:, turn, :], log_z[:, turn, :], ACT.Exp, scale=-1.0).then_inc(seed_done, 1)

            def step(b, k):
                c = b + 1
                if exists(b + 2):
                    high_q(b + 2, 0)
                    if exists(b - 1):
                        high_out(b - 1, 1)
                    high_q(b + 2, 1)
                if exists(b - 1):
                    probabilities(b, 0)
                    probabilities(b, 1)
                if not exists(c):
                    last_step(b, k)
                    return
                high_ip(b, k, 0)
                high_ip(b, k, 1)
                if not exists(b - 1):
                    probabilities(b, 0)
                    probabilities(b, 1)
                if not exists(b + 2):
                    high_out(b - 1, 1)
                probabilities(b, 2)
                probabilities(b, 3)
                if exists(b - 1):
                    high_out(b - 1, 2)
                if exists(b + 3):
                    act.wait_ge(q_ready, 2 * (b + 3))
                    split_x(b + 3)
                probabilities(b, 4)
                values(c, 1 - k)
                probabilities(b, 5)
                seed(b, k, 0)
                probabilities(b, 6)
                image_part(b, 0)
                probabilities(b, 7)
                image_part(b, 1)
                probabilities(b, 8)
                probabilities(b, 9)
                high_shift(c)
                image_exp(c)
                seed(b, k, 1)
                high_out(b, 0)
                seed(b, k, 2)

            def last_step(b, k):
                probabilities(b, 2)
                probabilities(b, 3)
                high_out(b - 1, 1)
                high_ip(b, k, 0)
                high_ip(b, k, 1)
                high_out(b - 1, 2)
                probabilities(b, 4)
                probabilities(b, 5)
                probabilities(b, 6)
                seed(b, k, 0)
                probabilities(b, 7)
                probabilities(b, 8)
                probabilities(b, 9)
                seed(b, k, 1)
                image_part(b, 0)
                image_part(b, 1)
                seed(b, k, 2)
                for chunk in range(XC):
                    high_out(b, chunk)

            def copy_v(b):
                act.wait_ge(va_ready, b + 1)
                copy(v_all[:, b], v_bank[b % 4][0:TEXT, 0:D].rearrange("p (h d) -> p h d", h=H)).then_inc(va_done, 1)

            high_q(0, 0)
            high_q(0, 1)
            act.wait_ge(q_ready, 2)
            split_x(1)
            act.wait_ge(high, len(splits))
            act.wait_ge(low, len(splits))
            for b in range(3):
                copy_v(b)
            act.wait_ge(vipn_ready, 1)
            copy(vipn[:], spare[1][0:B * IP, 0:DP]).then_inc(vipn_done, 1)
            copy_v(3)
            high_q(1, 0)
            high_q(1, 1)
            for b in range(4, B):
                copy_v(b)
            act.wait_ge(q_ready, 4)
            split_x(2)
            act.wait_ge(va_done, B)
            act.wait_ge(zeroed, 4)
            values(0, 0)
            high_shift(0)
            image_exp(0)
            every_step(act, step)

        @block.vector
        def _(dve):
            sub = lambda o, a, b: nc.vector.tensor_tensor(o, a, b, ALU.subtract)

            def split_x(c):
                dve.wait_ge(xh_done, c + 1)
                nc.vector.scalar_tensor_tensor(x_l[:, 2, :], x_h[:, 2, :], con[:, NEG_LOWER:NEG_LOWER + 1],
                                               x_raw[:, 2, :], ALU.mult, ALU.add).then_inc(xl_done, 1)

            def split(n):
                _, _, hi, lo, raw = splits[n]
                dve.wait_ge(high, n + 1)
                sub(lo, raw, hi).then_inc(low, 1)

            for n in range(K_SPLIT):
                split(n)
            dve.wait_ge(con_in, 16)
            split_x(0)

            dve.wait_ge(box_in, 16)
            steps = 0

            def chained(ins):
                nonlocal steps
                steps += 1
                ins.then_inc(mask_step, 1)
                dve.wait_ge(mask_step, steps)

            for t in range(QT):
                xg, yg = con[:, XG:XG + 1], con[:, YG + t:YG + t + 1]
                o = inside[:, t]
                chained(nc.vector.tensor_scalar(o, box[:, :, :, 0], xg, None, ALU.is_le))
                chained(nc.vector.scalar_tensor_tensor(o, box[:, :, :, 1], yg, o, ALU.is_le, ALU.mult))
                chained(nc.vector.scalar_tensor_tensor(o, box[:, :, :, 2], xg, o, ALU.is_ge, ALU.mult))
                chained(nc.vector.scalar_tensor_tensor(o, box[:, :, :, 3], yg, o, ALU.is_ge, ALU.mult))
                chained(nc.vector.tensor_reduce(some[:, t], o, X, ALU.max))
                nc.vector.tensor_scalar(mask[:, t, :, 0:BOX], some[:, t].unsqueeze(2).to_broadcast([P, B, BOX]),
                                        NEG, None, ALU.mult)
                nc.vector.tensor_scalar(mask[:, t, :, BOX:IP], o, -NEG, NEG, ALU.mult, ALU.add).then_inc(mask_ready, 1)

            split(Q_SPLIT - 1)
            split(V_SPLIT - 1)
            dve.wait_ge(kh_done, 1)
            for m in range(XC):
                ins = sub(kc_l[m][:, :, TEXT:KEYS], spare[0][:, 64 * m:64 * m + 64].rearrange("p (n b) -> p b n", b=B),
                          kc_h[m][:, :, TEXT:KEYS])
            ins.then_inc(kl_done, 1)
            for m in range(XC):
                for half in range(2):
                    b4 = slice(4 * half, 4 * half + 4)
                    dve.wait_ge(kh_done, 2 * m + half + 2)
                    sub(kc_l[m][:, b4, 0:TEXT], bank[2 * m + half][:, 0:448].rearrange("p (b n) -> p b n", b=4),
                        kc_h[m][:, b4, 0:TEXT]).then_inc(kl_done, 1)
            split(VIP_SPLIT - 1)
            dve.wait_ge(mask_ready, QT)

            def low_q(c, part):
                dve.wait_ge(qh_done, 2 * c + part + 1)
                if part == 0:
                    sub(q_l[:, 0:2, :], spare[0][:].rearrange("p (m n) -> p m n", m=2), q_h[:, 0:2, :]).then_inc(ql_done, 1)
                else:
                    sub(q_l[:, 2, :], spare[1][:, 0:S], q_h[:, 2, :]).then_inc(ql_done, 1)

            def read_a(c, n):
                t, g = n // GROUPS, n % GROUPS
                heads = slice(GROUP * g, GROUP * (g + 1))
                dve.wait_ge(a_ready, 2 * GROUPS * c + n + 1)
                if n == 0 and not (isinstance(c, int) and c == 0):
                    dve.wait_ge(shift_ready, c)
                    dve.wait_ge(ipd_done, c)
                s = a_bank[n % 2][:, 0:GROUP * KEYS].rearrange("p (h n) -> p h n", h=GROUP)
                nc.vector.tensor_reduce(negmax[:, t, :, 2 * g:2 * g + 2].rearrange("p a q -> p q a"),
                                        s[:, :, 0:TEXT].rearrange("p (q a) n -> p q a n", a=2), X, ALU.max,
                                        negate=True).then_inc(a_max, 1)
                nc.vector.tensor_tensor(ips[:, t, heads, :], s[:, :, TEXT:KEYS],
                                        mask[:, t, c, :].unsqueeze(1).to_broadcast([P, GROUP, IP]),
                                        ALU.add).then_inc(a_used, 1)

            def image_max(c):
                dve.wait_ge(a_used, 2 * GROUPS * (c + 1))
                nc.vector.tensor_reduce(ipm[:], ips[:], X, ALU.max).then_inc(ipm_done, 1)

            def low_shift(c):
                dve.wait_ge(sh_done, c + 1)
                sub(shift[:, 1], spare[1][0:H, 0:S], shift[:, 0]).then_inc(sl_done, 1)

            def image_sum(c):
                dve.wait_ge(ipe_done, c + 1)
                nc.vector.tensor_reduce(ipz[:], ipe[:], X, ALU.add).then_inc(ipz_done, 1)
                dve.wait_ge(ipz_done, c + 1)
                if not (isinstance(c, int) and c == 0):
                    dve.wait_ge(ipp_done, c)
                nc.vector.reciprocal(ipr[:], ipz[:]).then_inc(ipr_done, 1)

            def low_ip(b, k, part):
                dve.wait_ge(pih_done, 2 * b + part + 1)
                if part == 0:
                    sub(pip[64:P, 2, :], ip_bank(b, k, 0)[0:64, 0:S], pip[0:64, 2, :]).then_inc(pil_done, 1)
                else:
                    sub(pip[64:P, 0:2, :], ip_bank(b, k, 1)[0:64, :].rearrange("p (m n) -> p m n", m=2),
                        pip[0:64, 0:2, :]).then_inc(pil_done, 1)

            def normalise(b, k, c):
                dve.wait_ge(seed_done, XC * b + c + 1)
                r, turn = XC * b + c, (k + c) % 2
                nc.vector.tensor_tensor(zr[:], sums(b, k, c), rz[:, turn, :], ALU.mult).then_inc(zr_done, 1)
                dve.wait_ge(zr_done, r + 1)
                nc.vector.scalar_tensor_tensor(rz[:, turn, :], zr[:], -2.0, rz[:, turn, :],
                                               ALU.add, ALU.mult).then_inc(rz_done, 1)
                dve.wait_ge(rz_done, r + 1)
                if c == 0 and not (isinstance(b, int) and b == 0):
                    dve.wait_ge(on_done, XC * b)
                dve.wait_ge(oz_ready, r + 1)
                nc.vector.scalar_tensor_tensor(ot[:, c, :], oz_bank[turn][:, 0:S], -1.0, rz[:, turn, :],
                                               ALU.mult, ALU.mult).then_inc(ot_done, 1)

            def add_image(b, c):
                dve.wait_ge(ot_done, XC * b + c + 1)
                dve.wait_ge(oi_done, 2 * b + 1 + c // 2)
                nc.vector.tensor_tensor(on[:, c, :], ot[:, c, :], oi[:, c, :], ALU.add).then_inc(on_done, 1)

            def low_out(b, c):
                dve.wait_ge(onh_done, XC * b + c + 1)
                sub(on_l[:, c, :], on[:, c, :], on_h[:, c, :]).then_inc(onl_done, 1)

            def last_chunk_out(b):
                dve.wait_ge(onh_done, XC * (b + 1))
                if not (isinstance(b, int) and b == 0):
                    dve.wait_ge(out_ready, QT * b)
                nc.vector.scalar_tensor_tensor(on_l[:, 2, :], on_h[:, 2, :], con[:, NEG_SECOND:NEG_SECOND + 1],
                                               on[:, 2, :], ALU.mult, ALU.add).then_inc(onl_done, 1)

            def add_residual(b, t):
                dve.wait_ge(out_ready, QT * b + t + 1)
                if t == 0:
                    dve.wait_ge(xb_done, b + 1)
                    if not (isinstance(b, int) and b == 0):
                        dve.wait_ge(y_stored, 16 * b)
                nc.vector.tensor_tensor(y[:, t, :], spare[t][:, 0:D], xb[:, t, :], ALU.add).then_inc(y_done, 1)

            def step(b, k):
                c = b + 1
                reads = [n for n in range(2 * GROUPS) if exists(c)]

                def some_a(n):
                    for _ in range(n):
                        if reads:
                            read_a(c, reads.pop(0))

                if not exists(c):
                    dve.wait_ge(on_done, XC * (b - 1) + 2)
                    add_image(b - 1, 2)
                some_a(2)
                low_ip(b, k, 0)
                some_a(1)
                low_ip(b, k, 1)
                some_a(1)
                if exists(b + 2):
                    low_q(b + 2, 0)
                    low_q(b + 2, 1)
                some_a(1)
                if not exists(c):
                    dve.wait_ge(onl_done, XC * (b - 1) + 2)
                if exists(b - 1):
                    last_chunk_out(b - 1)
                some_a(5)
                if exists(c):
                    image_max(c)
                    low_shift(c)
                if exists(b + 3):
                    split_x(b + 3)
                if exists(b - 1):
                    add_residual(b - 1, 0)
                    add_residual(b - 1, 1)
                normalise(b, k, 0)
                if exists(c):
                    image_sum(c)
                    normalise(b, k, 1)
                    normalise(b, k, 2)
                else:
                    normalise(b, k, 1)
                    add_image(b, 0)
                    add_image(b, 1)
                    low_out(b, 0)
                    low_out(b, 1)
                    normalise(b, k, 2)
                    add_image(b, 2)

            def ones(k):
                dve.wait_ge(zeroed, k + 4)
                for ab in range(2):
                    nc.vector.tensor_copy(
                        ks[k][STACK:STACK + SHIFT, :, ab, :],
                        con[STACK:STACK + SHIFT, SHIFT_ROWS + ab:SHIFT_ROWS + ab + 1].unsqueeze(2)
                        .to_broadcast([SHIFT, PAIRS, KEYS])).then_inc(ones_set, 1)

            low_q(0, 0)
            low_q(0, 1)
            split(VIP_SPLIT)
            split_x(1)
            ones(0)
            ones(1)
            low_q(1, 0)
            low_q(1, 1)
            for n in range(2 * GROUPS):
                read_a(0, n)
            image_max(0)
            low_shift(0)
            split_x(2)
            image_sum(0)
            every_step(dve, step)
            last_chunk_out(B - 1)
            add_residual(B - 1, 0)
            add_residual(B - 1, 1)

        @block.gpsimd
        def _(pool):
            sub = lambda o, a, b: nc.gpsimd.tensor_tensor(o, a, b, ALU.subtract)
            for tile in (v[0], v[1], ipp, ks[0]):
                nc.gpsimd.memset(tile[:].bitcast(F32) if tile is ks[0] else tile[:], 0.0).then_inc(zeroed, 1)

            def split_x(c):
                pool.wait_ge(xh_done, c + 1)
                sub(x_l[:, 0:2, :], x_raw[:, 0:2, :], x_h[:, 0:2, :]).then_inc(xl_done, 1)

            def image_values(c):
                pool.wait_ge(vr_first_in if isinstance(c, int) and c == 0 else vr_in, 32)
                if not (isinstance(c, int) and c == 0):
                    pool.wait_ge(vip_done, c)
                nc.gpsimd.tensor_tensor(vm[:], vr[:, c], con[:, BLOCK:BLOCK + DP], ALU.mult).then_inc(vm_done, 1)
                if not (isinstance(c, int) and c == 0):
                    pool.wait_ge(oip_ready, 2 * c)
                pool.wait_ge(vm_done, c + 1)
                nc.gpsimd.tensor_tensor(vip_h[:], vm[:], con[:, BLOCK:BLOCK + DP], ALU.mult).then_inc(viph_done, 1)
                pool.wait_ge(viph_done, c + 1)
                sub(vip_l[:], vm[:], vip_h[:]).then_inc(vip_done, 1)

            def image_shift(c):
                pool.wait_ge(ipm_done, c + 1)
                if not (isinstance(c, int) and c == 0):
                    pool.wait_ge(ipe_done, c)
                nc.gpsimd.tensor_tensor(ipd[:], ips[:], ipm[:].unsqueeze(3).to_broadcast([P, QT, H, IP]),
                                        ALU.subtract).then_inc(ipd_done, 1)

            def image_norm(c):
                pool.wait_ge(ipr_done, c + 1)
                if not (isinstance(c, int) and c == 0):
                    pool.wait_ge(ipt_ready, 2 * c)
                nc.gpsimd.tensor_tensor(ipp[:, :, 0:H, :], ipe[:], ipr[:].unsqueeze(3).to_broadcast([P, QT, H, IP]),
                                        ALU.mult).then_inc(ipp_done, 1)

            def residual(b):
                pool.wait_ge(xres_in, 16 * (b + 1))
                if not (isinstance(b, int) and b == 0):
                    pool.wait_ge(y_done, QT * b)
                else:
                    pool.wait_ge(bias_in, 16)
                nc.gpsimd.tensor_tensor(xb[:], x_res[:], bias[:].unsqueeze(1).to_broadcast([P, QT, D]),
                                        ALU.add).then_inc(xb_done, 1)

            def output(b, c):
                pool.wait_ge(ot_done, XC * b + c + 1)
                pool.wait_ge(oi_done, 2 * b + 1 + c // 2)
                if c == 0 and not (isinstance(b, int) and b == 0):
                    pool.wait_ge(onl_done, XC * b)
                nc.gpsimd.tensor_tensor(on[:, c, :], ot[:, c, :], oi[:, c, :], ALU.add).then_inc(on_done, 1)
                if c < 2:
                    pool.wait_ge(onh_done, XC * b + c + 1)
                    sub(on_l[:, c, :], on[:, c, :], on_h[:, c, :]).then_inc(onl_done, 1)

            def step(b, k):
                if exists(b + 3):
                    split_x(b + 3)
                if exists(b + 1):
                    image_values(b + 1)
                    image_shift(b + 1)
                    output(b, 0)
                    image_norm(b + 1)
                    output(b, 1)
                    if exists(b + 2):
                        output(b, 2)
                residual(b)

            split_x(0)
            pool.wait_ge(k_ready, 7)
            nc.gpsimd.memset(ks[1][:].bitcast(F32), 0.0).then_inc(zeroed, 1)
            split_x(1)
            split_x(2)
            image_shift(0)
            image_norm(0)
            image_values(0)
            every_step(pool, step)


def kernel(x, ctx_2048, fside_Bx4x4_0, L0_xattn_w_q, L0_xattn_w_k, L0_xattn_w_v, L0_xattn_w_k_ip,
           L0_xattn_w_v_ip, L0_xattn_w_out, L0_xattn_b_out):
    import numpy as np
    import concourse.bacc as bacc
    from concourse.bass_utils import run_bass_kernel_spmd

    x, ctx_all, box = (np.ascontiguousarray(a) for a in (x, ctx_2048, fside_Bx4x4_0))
    wq, wk, wv, wk_ip, wv_ip, w_out, b_out = (np.ascontiguousarray(a) for a in (
        L0_xattn_w_q, L0_xattn_w_k, L0_xattn_w_v, L0_xattn_w_k_ip, L0_xattn_w_v_ip, L0_xattn_w_out, L0_xattn_b_out))

    def by_chunk(rows):
        return np.ascontiguousarray(rows.reshape(-1, P, rows.shape[1]).transpose(1, 0, 2))

    def padded(w):
        return np.pad(w, ((0, 0), (0, DP - D)))

    rows = np.r_[0:D, 2 * P:D]
    out_rows = np.r_[0:2 * P, np.concatenate([np.r_[h * DH:(h + 1) * DH, h * DH:(h + 1) * DH] for h in range(16, H)])]
    xT = x.transpose(0, 2, 1)[:, rows, :].reshape(B, XC, P, S).transpose(0, 2, 1, 3)
    arrays = {
        "xT": xT,
        "x": x,
        "ctxT": by_chunk(ctx_all[:, :TEXT].reshape(B * TEXT, C).T),
        "ctx_ipT": by_chunk(np.tile(ctx_all[:, TEXT:].transpose(2, 1, 0).reshape(C, IP * B), (1, 2))),
        "bbox": box.reshape(B * BOX * 4),
        "wq": by_chunk(padded(wq)[rows]),
        "wk": by_chunk(padded(wk)),
        "wv": by_chunk(wv),
        "wk_ip": by_chunk(padded(wk_ip)),
        "wv_ip": by_chunk(wv_ip[:, out_rows]),
        "w_out": by_chunk(w_out[out_rows]),
        "b_out": b_out,
        "consts": constants(),
    }
    nc = bacc.Bacc("TRN2", target_bir_lowering=False, num_devices=1)
    args = []
    for name, a in arrays.items():
        arrays[name] = a = np.ascontiguousarray(a)
        args.append(nc.dram_tensor(name, a.shape, mybir.dt.from_np(a.dtype), kind="ExternalInput").ap())
    args.append(nc.dram_tensor("out", (B, S, D), F32, kind="ExternalOutput").ap())
    build(nc, *args)
    r = run_bass_kernel_spmd(nc, [arrays], core_ids=[0])
    return r.results[0]["out"]
```
